# Optimizing a Trainium2 kernel written in Bass

```python
import numpy as np
import jax
import jax.numpy as jnp

def _softmax(x, axis=-1):
    return jax.nn.softmax(x, axis=axis)

def _gelu(x):
    return jax.nn.gelu(x, approximate=True)

def _silu(x):
    return jax.nn.silu(x)

def _sigmoid(x):
    return jax.nn.sigmoid(x)

def _layernorm(x, axis=-1, eps=1e-05):
    m = jnp.mean(x, axis=axis, keepdims=True)
    v = jnp.var(x, axis=axis, keepdims=True)
    return (x - m) / jnp.sqrt(v + eps)

def _scatter_add(tgt, idx, src, axis=0):
    return tgt.at[idx].add(src)

def _segment_sum(src, seg, n):
    return jax.ops.segment_sum(src, seg, n)
kernel_name = 'mk_early_fusion_d1_tok_img768_r4_c7b5cc'

def setup_inputs(seed: int=0):
    np.random.seed(seed)
    _w = jnp.asarray

    def _rec_inputs():
        import jax
        import jax.numpy as jnp
        _rk = jax.random.key(seed)
        x = -0.000209053 + 0.999977 * jax.random.normal(jax.random.fold_in(_rk, 1), (4, 64, 112, 112), jnp.float32)
        txt = -0.000113515 + 0.477431 * jax.random.normal(jax.random.fold_in(_rk, 2), (4, 512, 192), jnp.float32)
        return (x, txt)
    x, txt = _rec_inputs()

    def _L0_tok_setup():
        import jax, jax.numpy as jnp
        import numpy as np
        K = 3
        STRIDE = 2
        PAD = (K - 1) // 2
        key = jax.random.key(seed)
        k1, k2, k3 = jax.random.split(key, 3)
        B, C, H, W_ = (32, 64, 112, 112)
        DIM = 192
        x = jax.random.normal(k1, (B, C, H, W_), dtype=jnp.float32)
        W = jax.random.normal(k2, (DIM, C * K * K), dtype=jnp.float32) * 0.02
        b = jax.random.normal(k3, (DIM,), dtype=jnp.float32) * 0.02
        return {'x': x, 'W': W, 'b': b}
    _L0_tok_all = _L0_tok_setup()
    _L0_tok_in = {k: v for k, v in _L0_tok_all.items() if k in ('W', 'b')}
    del _L0_tok_all

    def _L0_attn_setup():
        import jax, jax.numpy as jnp
        import numpy as np
        import math
        EMBED_DIM = 192
        NUM_HEADS = 12
        N_QUBITS = 96
        D_K = N_QUBITS // NUM_HEADS
        key = jax.random.key(seed)
        k1, k2, k3 = jax.random.split(key, 3)
        x = jax.random.normal(k1, (8, 256, EMBED_DIM), dtype=jnp.float32)
        theta = jax.random.uniform(k2, (N_QUBITS,), dtype=jnp.float32, minval=-math.pi, maxval=math.pi)
        W_combine = jax.random.normal(k3, (EMBED_DIM, N_QUBITS), dtype=jnp.float32) / math.sqrt(N_QUBITS)
        return {'x': x, 'theta': theta, 'W_combine': W_combine}
    _L0_attn_all = _L0_attn_setup()
    _L0_attn_in = {k: v for k, v in _L0_attn_all.items() if k in ('theta', 'W_combine')}
    del _L0_attn_all

    def _L0_ffn_setup():
        import jax, jax.numpy as jnp
        import numpy as np
        B, S, H, D, E = (4, 512, 192, 256, 8)
        TOP_K = 2
        EPS = 1e-08
        LN_EPS = 1e-05

        def _gelu(t):
            return jax.nn.gelu(t, approximate=False)

        def _layer_norm(t, gamma, beta):
            mu = jnp.mean(t, axis=-1, keepdims=True)
            var = jnp.mean(jnp.square(t - mu), axis=-1, keepdims=True)
            return (t - mu) * jax.lax.rsqrt(var + LN_EPS) * gamma + beta
        key = jax.random.key(seed)
        ks = jax.random.split(key, 8)
        x = jax.random.normal(ks[0], (B, S, H), dtype=jnp.float32)
        w1 = jax.random.normal(ks[1], (H, H // 2), dtype=jnp.float32) * 0.02
        b1 = jnp.zeros((H // 2,), dtype=jnp.float32)
        w2 = jax.random.normal(ks[2], (H // 2, E), dtype=jnp.float32) * 0.02
        b2 = jnp.zeros((E,), dtype=jnp.float32)
        a_dn = float(np.sqrt(6.0 / (H + D)))
        a_up = float(np.sqrt(6.0 / (D + H)))
        down_w = jax.random.uniform(ks[3], (E, H, D), dtype=jnp.float32, minval=-a_dn, maxval=a_dn)
        down_b = jnp.zeros((E, D), dtype=jnp.float32)
        up_w = jax.random.uniform(ks[4], (E, D, H), dtype=jnp.float32, minval=-a_up, maxval=a_up)
        gamma = jnp.ones((H,), dtype=jnp.float32)
        beta = jnp.zeros((H,), dtype=jnp.float32)
        return {'x': x, 'w1': w1, 'b1': b1, 'w2': w2, 'b2': b2, 'down_w': down_w, 'down_b': down_b, 'up_w': up_w, 'gamma': gamma, 'beta': beta}
    _L0_ffn_all = _L0_ffn_setup()
    _L0_ffn_in = {k: v for k, v in _L0_ffn_all.items() if k in ('w1', 'b1', 'w2', 'b2', 'down_w', 'down_b', 'up_w', 'gamma', 'beta')}
    del _L0_ffn_all
    return {'x': x, 'txt': txt, 'L0_tok_W': _L0_tok_in['W'], 'L0_tok_b': _L0_tok_in['b'], 'L0_attn_theta': _L0_attn_in['theta'], 'L0_attn_W_combine': _L0_attn_in['W_combine'], 'L0_ffn_w1': _L0_ffn_in['w1'], 'L0_ffn_b1': _L0_ffn_in['b1'], 'L0_ffn_w2': _L0_ffn_in['w2'], 'L0_ffn_b2': _L0_ffn_in['b2'], 'L0_ffn_down_w': _L0_ffn_in['down_w'], 'L0_ffn_down_b': _L0_ffn_in['down_b'], 'L0_ffn_up_w': _L0_ffn_in['up_w'], 'L0_ffn_gamma': _L0_ffn_in['gamma'], 'L0_ffn_beta': _L0_ffn_in['beta']}

def reference(x, txt, L0_tok_W, L0_tok_b, L0_attn_theta, L0_attn_W_combine, L0_ffn_w1, L0_ffn_b1, L0_ffn_w2, L0_ffn_b2, L0_ffn_down_w, L0_ffn_down_b, L0_ffn_up_w, L0_ffn_gamma, L0_ffn_beta):
    import jax
    import jax.numpy as jnp

    def _L0_tok_ref(x, W, b):
        import jax, jax.numpy as jnp
        import numpy as np
        K = 3
        STRIDE = 2
        PAD = (K - 1) // 2
        dim = W.shape[0]
        C = x.shape[1]
        kernel = W.reshape(dim, C, K, K)
        y = jax.lax.conv_general_dilated(x, kernel, window_strides=(STRIDE, STRIDE), padding=[(PAD, PAD), (PAD, PAD)], dimension_numbers=('NCHW', 'OIHW', 'NCHW'))
        B, _, Hp, Wp = y.shape
        out = y.reshape(B, dim, Hp * Wp).transpose(0, 2, 1) + b
        return out

    def _L0_attn_ref(x, theta, W_combine):
        import jax, jax.numpy as jnp
        import numpy as np
        import math
        EMBED_DIM = 192
        NUM_HEADS = 12
        N_QUBITS = 96
        D_K = N_QUBITS // NUM_HEADS
        B, S, _ = x.shape
        xs = x[..., :N_QUBITS]
        q_vecs = jnp.cos(xs) * jnp.cos(theta)
        q = q_vecs.reshape(B, S, NUM_HEADS, D_K).transpose(0, 2, 1, 3)
        scores = jnp.einsum('bhsd,bhtd->bhst', q, q) / math.sqrt(D_K)
        probs = jax.nn.softmax(scores, axis=-1)
        attn = jnp.einsum('bhst,bhtd->bhsd', probs, q)
        attn = attn.transpose(0, 2, 1, 3).reshape(B, S, N_QUBITS)
        return attn @ W_combine.T

    def _L0_ffn_ref(x, w1, b1, w2, b2, down_w, down_b, up_w, gamma, beta):
        import jax, jax.numpy as jnp
        import numpy as np
        B, S, H, D, E = (4, 512, 192, 256, 8)
        TOP_K = 2
        EPS = 1e-08
        LN_EPS = 1e-05

        def _gelu(t):
            return jax.nn.gelu(t, approximate=False)

        def _layer_norm(t, gamma, beta):
            mu = jnp.mean(t, axis=-1, keepdims=True)
            var = jnp.mean(jnp.square(t - mu), axis=-1, keepdims=True)
            return (t - mu) * jax.lax.rsqrt(var + LN_EPS) * gamma + beta
        logits = _gelu(x @ w1 + b1) @ w2 + b2
        routing = jax.nn.softmax(logits, axis=-1)
        topv, topi = jax.lax.top_k(routing, TOP_K)
        sparse = jnp.sum(jax.nn.one_hot(topi, E, dtype=routing.dtype) * topv[..., None], axis=-2)
        sparse = sparse / (jnp.sum(sparse, axis=-1, keepdims=True) + EPS)
        z = _gelu(jnp.einsum('bsh,ehd->bsed', x, down_w) + down_b)
        expert_out = jnp.einsum('bsed,edh->bseh', z, up_w)
        moe_out = jnp.einsum('bseh,bse->bsh', expert_out, sparse)
        return _layer_norm(x + moe_out, gamma, beta)
    h = _L0_tok_ref(x, L0_tok_W, L0_tok_b)
    h = jnp.concatenate([h, txt], axis=1)
    h = h + _L0_attn_ref(_layernorm(h, axis=-1), L0_attn_theta, L0_attn_W_combine)
    h = h + _L0_ffn_ref(_layernorm(h, axis=-1), L0_ffn_w1, L0_ffn_b1, L0_ffn_w2, L0_ffn_b2, L0_ffn_down_w, L0_ffn_down_b, L0_ffn_up_w, L0_ffn_gamma, L0_ffn_beta)
    return h

_drawn_inputs = setup_inputs


def setup_inputs(seed=0):
    import zlib

    import numpy as np

    out = dict(_drawn_inputs(seed))
    spreads = {'L0_ffn_b1': (0.0, 0.1),
     'L0_ffn_b2': (0.0, 0.1),
     'L0_ffn_down_b': (0.0, 0.28),
     'L0_ffn_gamma': (1.0, 0.2),
     'L0_ffn_beta': (0.0, 0.1)}
    factors = {}
    for name, (base, spread) in spreads.items():
        noise = np.random.default_rng([zlib.crc32(name.encode()), seed]).standard_normal(out[name].shape)
        drawn = base * np.exp(spread * noise) if base else spread * noise
        out[name] = jnp.asarray(drawn.astype(out[name].dtype))
    for name, factor in factors.items():
        out[name] = (out[name] * factor).astype(out[name].dtype)
    return out
```

```python
import math
from contextlib import ExitStack

import numpy as np
import concourse.bass as bass
from concourse import mybir

F32 = mybir.dt.float32
F16 = mybir.dt.float16
I32 = mybir.dt.int32
ALU = mybir.AluOpType
ACT = mybir.ActivationFunctionType
AX_X = mybir.AxisListType.X
ds = bass.ds

P = 128
B, C_IN, HW = 4, 64, 112
DIM = 192
HALF = DIM // 2
SIDE = HW // 2
IMG = SIDE * SIDE
TXT = 512
T = IMG + TXT
NTOK = B * T
HEADS, DK = 12, 8
GROUPS, LANES = 3, 4
EXPERTS, EXP_D = 8, 256
Q_SCALE = 16.0
LN_EPS = 1e-5
GATE_EPS = 1e-8
RSQRT_MAGIC = float(0x5F3759DF)
ROUND_MAGIC = 1.5 * 2.0 ** 23
TWO_PI_HI = 6.28125
TWO_PI_LO = 2 * math.pi - TWO_PI_HI

BANDS = 7
UNITS = BANDS + 1
TILES = 4
TILE_IMG = 2 * SIDE
BAND_TOK = TILES * TILE_IMG
BAND_ROWS = 16
XROWS = BAND_ROWS // 2 + 1

CH = 456
CHUNKS = T // CH
NCHUNK = B * CHUNKS
KT = -(-T // P)
LAST_KEYS = T - (KT - 1) * P
T_PAD = KT * P
PAIRS = (KT - 1) // 2
TRIPLE = 3
VROW = LANES * 32 + DK

ST = 3
SN = ST * P
NSUPER = NTOK // SN


def wait_apart(engine, sem, value, idle):
    engine.wait_ge(sem, value)
    engine.sem_inc(idle, 1)


class Steps:

    def __init__(self, engine, sem, base=0):
        self.engine, self.sem, self.base, self.n = engine, sem, base, 0

    def __call__(self, ins):
        ins.then_inc(self.sem, 1)
        self.n += 1
        return ins

    def settle(self, idle=None):
        if idle is None:
            self.engine.wait_ge(self.sem, self.base + self.n)
        else:
            wait_apart(self.engine, self.sem, self.base + self.n, idle)


def newton_rsqrt(nc, do, y, x, t, ti):
    do.settle()
    do(nc.vector.tensor_scalar(ti, x.bitcast(I32), 1, None, ALU.logical_shift_right))
    do.settle()
    do(nc.vector.tensor_scalar(y.bitcast(I32), ti, -1.0, RSQRT_MAGIC, ALU.mult, ALU.add))
    for _ in range(3):
        do.settle()
        do(nc.vector.scalar_tensor_tensor(t, y, -0.5, y, ALU.mult, ALU.mult))
        do.settle()
        do(nc.vector.tensor_tensor(t, t, x, ALU.mult))
        do.settle()
        do(nc.vector.scalar_tensor_tensor(y, t, 1.5, y, ALU.add, ALU.mult))


def layer_stats(nc, do, idle, src, n, rows, stats, mv, vare, rstd, tmp, tmpi):
    do.settle()
    for i in range(n):
        do(nc.vector.bn_stats(stats[0:rows, i, :], src[0:rows, i, :]))
    do.settle(idle)
    for i in range(n):
        do(nc.vector.bn_aggr(mv[0:rows, i, :], stats[0:rows, i, :]))
    do.settle()
    do(nc.vector.tensor_scalar(vare[0:rows, 0:n], mv[0:rows, 0:n, 1], LN_EPS, None, ALU.add))
    newton_rsqrt(nc, do, rstd[0:rows, 0:n], vare[0:rows, 0:n], tmp[0:rows, 0:n], tmpi[0:rows, 0:n])
    do.settle()


def cos_argument(nc, do, arg, x, k, r):
    do.settle()
    do(nc.vector.tensor_scalar(k, x, 1.0 / (2 * math.pi), ROUND_MAGIC, ALU.mult, ALU.add))
    do.settle()
    do(nc.vector.tensor_scalar(k, k, ROUND_MAGIC, None, ALU.subtract))
    do.settle()
    do(nc.vector.scalar_tensor_tensor(r, k, -TWO_PI_HI, x, ALU.mult, ALU.add))
    do.settle()
    do(nc.vector.scalar_tensor_tensor(r, k, -TWO_PI_LO, r, ALU.mult, ALU.add))
    do.settle()
    do(nc.vector.scalar_tensor_tensor(arg, r, -1.0, r, ALU.mult, ALU.min))


def tokens_phase(nc, x, txt, tok_w, tok_b, theta, ident16, h_s, q_s, kt_s, qt_s):
    with ExitStack() as ctx:
        def sb(name, shape, dt=F32):
            return ctx.enter_context(nc.sbuf_tensor(name, shape, dt))

        def ps(name, shape, dt=F32):
            return ctx.enter_context(nc.psum_tensor(name, shape, dt))

        def sem(name):
            return ctx.enter_context(nc.semaphore(name))

        xband = {k: sb(f"xband_{k}", [P, XROWS, HW]) for k in ("top", "odd", "even")}
        planes = [sb(f"planes{i}", [P, 3, XROWS, SIDE]) for i in range(2)]
        w01 = sb("w01", [P, 3, DIM])
        w2 = sb("w2_taps", [P, 3, DIM])
        bias = sb("tok_bias", [P, DIM])
        id16 = sb("id16", [P, P], F16)
        theta_sb = sb("theta_sb", [P, HALF])
        cos_theta = sb("cos_theta", [P, HALF])
        half_pi = sb("half_pi", [P, 1])
        h = [sb(f"h{i}", [P, TILES, DIM]) for i in range(2)]
        q = [sb(f"q{i}", [P, TILES, HALF]) for i in range(2)]
        q_hi = [sb(f"q_hi{i}", [P, TILES, HALF], F16) for i in range(2)]
        q_lo = [sb(f"q_lo{i}", [P, TILES, HALF], F16) for i in range(2)]
        k_form = [sb(f"k_form{i}", [P, TILES, GROUPS * P], F16) for i in range(2)]
        q_form = [sb(f"q_form{i}", [P, TILES, GROUPS * P], F16) for i in range(2)]
        k_out = [sb(f"k_out{i}", [P, GROUPS, TXT], F16) for i in range(2)]
        q_out = [sb(f"q_out{i}", [P, GROUPS, TXT], F16) for i in range(2)]
        normed = sb("normed", [P, TILES, HALF])
        rounds = sb("rounds", [P, TILES, HALF])
        rest = sb("rest", [P, TILES, HALF])
        arg = [sb(f"arg{i}", [P, TILES, HALF]) for i in range(2)]
        sine = [sb(f"sine{i}", [P, TILES, HALF]) for i in range(2)]
        stats = sb("stats", [P, TILES, 6])
        mv = sb("mv", [P, TILES, 2])
        vare, rstd, tmp = (sb(n, [P, TILES]) for n in ("vare", "rstd", "tmp"))
        tmpi = sb("tmpi", [P, TILES], I32)
        h_ps = [ps(f"h_ps{i}", [P, TILES, 256]) for i in range(2)]
        k_ps = ps("k_ps", [P, 4, 512], F16)
        q_ps = ps("q_ps", [P, 4, 512], F16)

        consts_loaded = sem("consts_loaded")
        cleared = sem("cleared")
        theta_arg = sem("theta_arg")
        theta_sin = sem("theta_sin")
        x_loaded = {k: sem(f"x_loaded_{k}") for k in xband}
        txt_loaded = sem("txt_loaded")
        planes_pool = sem("planes_pool")
        planes_act = sem("planes_act")
        conv_done = sem("conv_done")
        h_evacuated = sem("h_evacuated")
        h_ready = sem("h_ready")
        arg_ready = sem("arg_ready")
        sine_ready = sem("sine_ready")
        split_ready = sem("split_ready")
        forms_ready = sem("forms_ready")
        transposed = sem("transposed")
        t_evacuated = sem("t_evacuated")
        stored = [sem(f"stored{i}") for i in range(2)]
        dve_steps = sem("dve_steps")
        idle = sem("idle")

        BAND_DMAS = 32
        UNIT_STORES = 4 * 16
        FORM_STEPS = 4

        def rows_of(k):
            return P if k == UNITS - 1 else TILE_IMG

        def buffer_of(k):
            return "top" if k == 0 else ("odd", "even")[(k - 1) % 2]

        def build_plane(eng, copy, built, b, k, kx, wait):
            if wait:
                loads = b if k == 0 else b * 3 + (k - 1) // 2
                wait_apart(eng, x_loaded[buffer_of(k)], loads * BAND_DMAS + BAND_DMAS, idle)
                wait_apart(eng, conv_done, b * BANDS + max(k + 1, 2), idle)
            left = 1 if kx == 0 else 0
            first = 1 if kx == 0 else kx - 1
            copy(planes[k % 2][:, kx, :, left:SIDE],
                 xband[buffer_of(k)][:, :, first:first + 2 * (SIDE - left) - 1:2]).then_inc(built, 1)

        block = ctx.enter_context(nc.Block())

        @block.sync
        def _(sp):
            for kx in range(3):
                for ky, dst in ((0, w01[0:C_IN, kx, :]), (1, w01[C_IN:P, kx, :]), (2, w2[0:C_IN, kx, :])):
                    sp.dma_start(dst, tok_w[ky, kx]).then_inc(consts_loaded, 16)
            sp.dma_start(bias[:], tok_b.partition_broadcast(P)).then_inc(consts_loaded, 16)
            sp.dma_start(theta_sb[:], theta.partition_broadcast(P)).then_inc(consts_loaded, 16)
            sp.dma_start(id16[:], ident16).then_inc(consts_loaded, 16)
            sp.wait_ge(cleared, 6)

            def load_band(b, k, where, built):
                wait_apart(sp, planes_act, b * BANDS + built + 2, idle)
                wait_apart(sp, planes_pool, (b * BANDS + built + 2) * 2, idle)
                rows = x[ds(b, 1)].rearrange("b c (r two) w -> (b c) two r w", two=2)
                above = 1 if where == "top" else 0
                half = BAND_ROWS // 2
                sp.dma_start(xband[where][0:C_IN, above:XROWS, :],
                             rows[:, 1, k * half - 1 + above:(k + 1) * half, :]).then_inc(x_loaded[where], 16)
                sp.dma_start(xband[where][C_IN:P, 0:half, :],
                             rows[:, 0, k * half:(k + 1) * half, :]).then_inc(x_loaded[where], 16)

            with sp.Fori(0, B) as b:
                load_band(b, 0, "top", -1)
                for k in range(1, BANDS):
                    load_band(b, k, ("odd", "even")[(k - 1) % 2], k - 1 if k > 2 else k - 2)
                wait_apart(sp, stored[1], b * (4 * UNIT_STORES) + 4 * UNIT_STORES, idle)
                sp.dma_start(h[1][:], txt[ds(b, 1)].rearrange("b (t p) d -> p (b t) d", p=P)).then_inc(txt_loaded, 16)

        @block.gpsimd
        def _(pool):
            for k in ("top", "odd", "even"):
                nc.gpsimd.memset(xband[k][:], 0.0).then_inc(cleared, 1)
            for par in range(2):
                nc.gpsimd.memset(planes[par][:, 0, :, 0], 0.0).then_inc(cleared, 1)

            def expand(b, k):
                n, par, rows = b * UNITS + k, k % 2, rows_of(k)
                wait_apart(pool, split_ready, n + 1, idle)
                wait_apart(pool, transposed, n + 1, idle)
                hi = q_hi[par][0:rows].rearrange("p t (h d) -> p (t h) d", d=DK).unsqueeze(2)
                lo = q_lo[par][0:rows].rearrange("p t (h d) -> p (t h) d", d=DK).unsqueeze(2)
                both = [rows, TILES * HEADS, 2, DK]
                kf = k_form[par][0:rows].rearrange("p t (h r d) -> p (t h) r d", r=4, d=DK)
                qf = q_form[par][0:rows].rearrange("p t (h r d) -> p (t h) r d", r=4, d=DK)
                nc.gpsimd.tensor_copy(kf[:, :, 0:2, :], hi.broadcast_to(both)).then_inc(forms_ready, 1)
                nc.gpsimd.tensor_copy(kf[:, :, 2:4, :], lo.broadcast_to(both)).then_inc(forms_ready, 1)
                nc.gpsimd.tensor_copy(qf[:, :, 0:4:2, :], hi.broadcast_to(both)).then_inc(forms_ready, 1)
                nc.gpsimd.tensor_copy(qf[:, :, 1:4:2, :], lo.broadcast_to(both)).then_inc(forms_ready, 1)

            with pool.Fori(0, B) as b:
                for kx in (1, 2):
                    build_plane(pool, nc.gpsimd.tensor_copy, planes_pool, b, 0, kx, wait=(kx == 1))
                for k in range(UNITS):
                    if k + 1 < BANDS:
                        for kx in (1, 2):
                            build_plane(pool, nc.gpsimd.tensor_copy, planes_pool, b, k + 1, kx, wait=(kx == 1))
                    expand(b, k)

        @block.scalar
        def _(act):
            nc.scalar.preload_act_table(ACT.Sin)
            act.wait_ge(theta_arg, 1)
            nc.scalar.activation(cos_theta[:], theta_sb[:], ACT.Sin, bias=half_pi[:, 0:1]).then_inc(theta_sin, 1)

            def take_sine(b, k):
                n, par, rows = b * UNITS + k, k % 2, rows_of(k)
                act.wait_ge(arg_ready, n + 1)
                nc.scalar.activation(sine[par][0:rows], arg[par][0:rows], ACT.Sin,
                                     bias=half_pi[0:rows, 0:1]).then_inc(sine_ready, 1)

            def evacuate(b, k):
                n, par, rows = b * UNITS + k, k % 2, rows_of(k)
                tok = TILES * rows
                act.wait_ge(transposed, n + 3)
                act.wait_ge(stored[par], (b * 4 + k // 2) * UNIT_STORES + UNIT_STORES)
                nc.scalar.activation(k_out[par][:, :, 0:tok], k_ps[:, 0:GROUPS, 0:tok], ACT.Copy).then_inc(t_evacuated, 1)
                nc.scalar.activation(q_out[par][:, :, 0:tok], q_ps[:, 0:GROUPS, 0:tok], ACT.Copy).then_inc(t_evacuated, 1)
                act.wait_ge(t_evacuated, n * 2 + 4)
                at = k * BAND_TOK
                for src, dst in ((k_out, kt_s), (q_out, qt_s)):
                    act.dma_start(dst[ds(b, 1), :, :, at:at + tok].rearrange("b p g t -> (b p) g t"),
                                  src[par][:, :, 0:tok]).then_inc(stored[par], 16)
                act.wait_ge(split_ready, n + 1)
                for src, dst in ((h, h_s), (q, q_s)):
                    act.dma_start(dst[ds(b * T + at, tok), :].rearrange("(t p) d -> p t d", p=rows),
                                  src[par][0:rows]).then_inc(stored[par], 16)

            with act.Fori(0, B) as b:
                build_plane(act, nc.scalar.copy, planes_act, b, 0, 0, wait=True)
                build_plane(act, nc.scalar.copy, planes_act, b, 1, 0, wait=True)
                take_sine(b, 0)
                for k in range(1, UNITS):
                    if k + 1 < BANDS:
                        build_plane(act, nc.scalar.copy, planes_act, b, k + 1, 0, wait=True)
                    take_sine(b, k)
                    evacuate(b, k - 1)
                evacuate(b, UNITS - 1)
            for par in range(2):
                act.wait_ge(stored[par], (4 * B + 1) * UNIT_STORES)

        @block.vector
        def _(dve):
            pre = Steps(dve, dve_steps)
            nc.vector.memset(w2[C_IN:P, :, :], 0.0).then_inc(cleared, 1)
            pre(nc.vector.memset(half_pi[:], math.pi / 2))
            dve.wait_ge(consts_loaded, 12 * 16)
            flat = (rounds[:, 0, :], rest[:, 0, :])
            cos_argument(nc, pre, theta_sb[:], theta_sb[:], *flat)
            pre.settle()
            dve.sem_inc(planes_act, 2)
            dve.sem_inc(planes_pool, 4)
            dve.sem_inc(conv_done, 2)
            dve.sem_inc(h_evacuated, 2)
            dve.sem_inc(t_evacuated, 2)
            dve.sem_inc(transposed, 2)
            dve.sem_inc(forms_ready, 2 * FORM_STEPS)
            dve.sem_inc(stored[0], UNIT_STORES)
            dve.sem_inc(stored[1], UNIT_STORES)
            dve.sem_inc(theta_arg, 1)
            dve.wait_ge(theta_sin, 1)
            pre(nc.vector.tensor_scalar(cos_theta[:], cos_theta[:], Q_SCALE, None, ALU.mult))

            def front(b, k, do):
                n, par, rows = b * UNITS + k, k % 2, rows_of(k)
                dve.wait_ge(stored[par], (b * 4 + k // 2) * UNIT_STORES + UNIT_STORES)
                if k < BANDS:
                    dve.wait_ge(conv_done, b * BANDS + k + 3)
                    ins = nc.vector.tensor_tensor(h[par][0:rows], h_ps[k % 2][0:rows, :, 0:DIM],
                                                  bias[0:rows].unsqueeze(1).broadcast_to([rows, TILES, DIM]), ALU.add)
                    ins.then_inc(h_evacuated, 1)
                    dve.wait_ge(h_evacuated, b * BANDS + k + 3)
                else:
                    dve.wait_ge(txt_loaded, b * 16 + 16)
                layer_stats(nc, do, idle, h[par], TILES, rows, stats, mv, vare, rstd, tmp, tmpi)
                for t in range(TILES):
                    do(nc.vector.tensor_scalar(normed[0:rows, t, :], h[par][0:rows, t, 0:HALF], mv[0:rows, t, 0:1],
                                               rstd[0:rows, t:t + 1], ALU.subtract, ALU.mult))
                cos_argument(nc, do, arg[par][0:rows], normed[0:rows], rounds[0:rows], rest[0:rows])
                do.settle()
                dve.sem_inc(arg_ready, 1)

            def back(b, k, do):
                n, par, rows = b * UNITS + k, k % 2, rows_of(k)
                dve.wait_ge(sine_ready, n + 1)
                do(nc.vector.tensor_tensor(q[par][0:rows], sine[par][0:rows],
                                           cos_theta[0:rows].unsqueeze(1).broadcast_to([rows, TILES, HALF]), ALU.mult))
                do.settle()
                dve.wait_ge(forms_ready, n * FORM_STEPS + FORM_STEPS)
                do(nc.vector.tensor_copy(q_hi[par][0:rows], q[par][0:rows]))
                do.settle()
                do(nc.vector.tensor_tensor(q_lo[par][0:rows], q[par][0:rows], q_hi[par][0:rows], ALU.subtract))
                do.settle()
                dve.sem_inc(split_ready, 1)

            UNIT_STEPS = 3 * TILES + 1 + 11 + 5 + 3
            with dve.Fori(0, B) as b:
                do = Steps(dve, dve_steps, b * (UNITS * UNIT_STEPS) + pre.n)
                front(b, 0, do)
                for k in range(1, UNITS):
                    front(b, k, do)
                    back(b, k - 1, do)
                back(b, UNITS - 1, do)
                assert do.n == UNITS * UNIT_STEPS

        @block.tensor
        def _(pe):
            pe.wait_ge(consts_loaded, 12 * 16)
            pe.wait_ge(cleared, 6)

            def convolve(b, k):
                pe.wait_ge(planes_act, b * BANDS + k + 3)
                pe.wait_ge(planes_pool, (b * BANDS + k + 3) * 2)
                pe.wait_ge(h_evacuated, b * BANDS + max(k + 1, 2))
                for t in range(TILES):
                    for m in range(6):
                        oy, kx, w = m // 3, m % 3, (w01, w2)[m // 3]
                        at = (2 * t + oy) * SIDE
                        plane = planes[k % 2][:, kx].rearrange("p r c -> p (r c)")
                        last = nc.tensor.matmul(h_ps[k % 2][0:TILE_IMG, t, 0:DIM], plane[:, at:at + TILE_IMG], w[:, kx, :],
                                                start=(m == 0), stop=(m == 5))
                last.then_inc(conv_done, 1)

            def transpose(b, k):
                n, par, rows = b * UNITS + k, k % 2, rows_of(k)
                pe.wait_ge(forms_ready, (n + 3) * FORM_STEPS)
                pe.wait_ge(t_evacuated, n * 2 + 2)
                for form, out in ((k_form, k_ps), (q_form, q_ps)):
                    for t in range(TILES):
                        for g in range(GROUPS):
                            last = nc.tensor.transpose(out[:, g, t * rows:(t + 1) * rows],
                                                       form[par][0:rows, t, g * P:(g + 1) * P], id16[0:rows, 0:rows])
                last.then_inc(transposed, 1)

            with pe.Fori(0, B) as b:
                convolve(b, 0)
                for k in range(1, BANDS):
                    convolve(b, k)
                    transpose(b, k - 1)
                transpose(b, BANDS - 1)
                transpose(b, UNITS - 1)


def attention_phase(nc, q_s, kt_s, qt_s, ot_s):
    UNITS_T = GROUPS * LANES
    TRIPLES = UNITS_T // TRIPLE
    E_SCALE = 1.0 / (Q_SCALE * Q_SCALE * math.sqrt(DK))
    K_BUF, Q_BUF, V_BUF = GROUPS * T_PAD, UNITS_T * CH, KT * HALF
    with ExitStack() as ctx:
        def sb(name, shape, dt=F32):
            return ctx.enter_context(nc.sbuf_tensor(name, shape, dt))

        def ps(name, shape, dt=F32):
            return ctx.enter_context(nc.psum_tensor(name, shape, dt))

        def sem(name):
            return ctx.enter_context(nc.semaphore(name))

        keys = sb("keys", [P, 2 * K_BUF], F16)
        queries = sb("queries", [P, 2 * Q_BUF], F16)
        values = sb("values", [P, 2 * V_BUF])
        v_tile = [sb(f"v_tile{i}", [P, GROUPS * VROW]) for i in range(3)]
        probs = sb("probs", [P, UNITS_T, CH])
        out_sb = sb("out_sb", [P, 2 * CH])
        zeros = sb("zeros", [P, CH], F16)
        scores = [ps(f"scores{i}", [P, TRIPLE, 512]) for i in range(2)]
        out_ps = ps("out_ps", [P, 512])

        cleared = sem("att_cleared")
        keys_loaded = sem("keys_loaded")
        values_loaded = sem("values_loaded")
        queries_loaded = sem("queries_loaded")
        scores_ready = sem("scores_ready")
        probs_ready = sem("probs_ready")
        pv_done = sem("pv_done")
        v_ready = sem("v_ready")
        out_evacuated = sem("out_evacuated")
        out_stored = sem("out_stored")
        idle = sem("idle_a")
        AHEAD = 4
        CLEARS = 8
        Q_DMAS = LANES * 16

        block = ctx.enter_context(nc.Block())

        def chunk_done(c):
            return (c + 1) * (KT * GROUPS) + AHEAD

        @block.sync
        def _(sp):
            sp.wait_ge(cleared, CLEARS)

            def load_batch(b):
                par = b % 2
                kdst = keys[:, par * K_BUF:(par + 1) * K_BUF].rearrange("p (g t) -> p g t", g=GROUPS)
                sp.dma_start(kdst[:, :, 0:T], kt_s[b]).then_inc(keys_loaded, 16)
                wait_apart(sp, keys_loaded, (b + 1) * 16, idle)
                vdst = values[:, par * V_BUF:(par + 1) * V_BUF].rearrange("p (t d) -> p t d", d=HALF)
                full = (KT - 1) * P
                sp.dma_start(vdst[:, 0:KT - 1, :],
                             q_s[b * T:b * T + full, :].rearrange("(t p) d -> p t d", p=P)).then_inc(values_loaded, 16)
                sp.dma_start(vdst[0:LAST_KEYS, KT - 1, :], q_s[b * T + full:(b + 1) * T, :]).then_inc(values_loaded, 16)
                wait_apart(sp, values_loaded, (b + 1) * 32, idle)

            def load_queries(c):
                buf = (c % 2) * Q_BUF
                for j in range(LANES):
                    lane = slice(32 * j, 32 * j + 32)
                    dst = queries[lane, ds(buf, Q_BUF)].rearrange("p (g j t) -> p g j t", g=GROUPS, j=LANES)[:, :, j, :]
                    src = qt_s[ds(c // CHUNKS, 1), lane].rearrange("b p g t -> (b p) g t")[:, :, ds(c % CHUNKS * CH, CH)]
                    sp.dma_start(dst, src).then_inc(queries_loaded, 16)
                wait_apart(sp, queries_loaded, c * Q_DMAS + Q_DMAS, idle)

            def store_out(c):
                wait_apart(sp, out_evacuated, c + 2, idle)
                sp.dma_start(ot_s[:, ds(c * CH, CH)], out_sb[:, ds(c % 2 * CH, CH)]).then_inc(out_stored, 16)
                wait_apart(sp, out_stored, c * 16 + 48, idle)

            load_batch(0)
            load_queries(0)
            load_queries(1)
            load_batch(1)
            for b in range(B):
                if 1 <= b < B - 1:
                    load_batch(b + 1)
                with sp.Fori(b * CHUNKS + 2, min((b + 1) * CHUNKS + 2, NCHUNK)) as c:
                    wait_apart(sp, pv_done, chunk_done(c - 2), idle)
                    load_queries(c)
                    store_out(c - 2)
            sp.sem_inc(queries_loaded, Q_DMAS)
            sp.sem_inc(keys_loaded, 16)
            store_out(NCHUNK - 2)
            store_out(NCHUNK - 1)

        @block.vector
        def _(dve):
            for buf in (queries, keys, zeros, *v_tile):
                nc.vector.memset(buf[:], 0.0).then_inc(cleared, 1)
            dve.wait_ge(cleared, 6)
            ones = []
            for i, rows in ((0, P), (1, P), (2, LAST_KEYS)):
                for g in range(GROUPS):
                    strips = v_tile[i][0:rows, g * P:(g + 1) * P].rearrange("p (j x) -> p j x", x=32)
                    ones.append(nc.vector.memset(strips[:, :, 3 * DK + g], Q_SCALE))
            ones[-2].then_inc(cleared, 1)
            ones[-1].then_inc(cleared, 1)
            dve.sem_inc(out_evacuated, 1)
            dve.sem_inc(out_stored, 32)
            dve.sem_inc(pv_done, AHEAD)
            with dve.Fori(0, NCHUNK) as c:
                dve.wait_ge(pv_done, chunk_done(c))
                dve.wait_ge(out_stored, c * 16 + 16)
                nc.vector.tensor_copy(out_sb[:, ds(c % 2 * CH, CH)], out_ps[:, 0:CH]).then_inc(out_evacuated, 1)

        @block.gpsimd
        def _(pool):
            pool.wait_ge(cleared, CLEARS)

            def place_values(n, tile, rows, start):
                wait_apart(pool, pv_done, n * GROUPS + (AHEAD - GROUPS), idle)
                dst = v_tile[tile][0:rows].rearrange("p (g r) -> p g r", r=VROW)[:, :, 0:P]
                dst = dst.rearrange("p g (j x) -> p g j x", x=32)[:, :, :, 0:DK]
                src = values[0:rows, ds(start, HALF)].rearrange("p (g j d) -> p g j d", g=GROUPS, j=LANES)
                nc.gpsimd.tensor_copy(dst, src).then_inc(v_ready, 1)

            with pool.Fori(0, NCHUNK) as c:
                buf = (c // CHUNKS % 2) * V_BUF
                wait_apart(pool, values_loaded, (c // CHUNKS) * 32 + 32, idle)
                with pool.Fori(0, PAIRS) as i:
                    for x in range(2):
                        place_values(c * KT + i * 2 + x, x, P, buf + i * (2 * HALF) + x * HALF)
                place_values(c * KT + KT - 1, 2, LAST_KEYS, buf + (KT - 1) * HALF)

        @block.scalar
        def _(act):
            nc.scalar.preload_act_table(ACT.Exp)

            def exps(n):
                for k in range(TRIPLES):
                    act.wait_ge(scores_ready, n * TRIPLES + (k + 1))
                    last_group = min((TRIPLE * k + TRIPLE - 1) // LANES, GROUPS - 1)
                    act.wait_ge(pv_done, n * GROUPS + (last_group + 1 + AHEAD - GROUPS))
                    nc.scalar.activation(probs[:, TRIPLE * k:TRIPLE * (k + 1), :], scores[k % 2][:, :, 0:CH],
                                         ACT.Exp, scale=E_SCALE).then_inc(probs_ready, 1)

            with act.Fori(0, NCHUNK) as c:
                with act.Fori(0, PAIRS) as i:
                    exps(c * KT + i * 2)
                    exps(c * KT + i * 2 + 1)
                exps(c * KT + KT - 1)

        @block.tensor
        def _(pe):
            def score(k, key_at, query_at):
                for m in range(TRIPLE):
                    u = TRIPLE * k + m
                    last = nc.tensor.matmul(scores[k % 2][:, m, 0:CH], keys[:, ds(key_at + (u // LANES) * T_PAD, P)],
                                            queries[:, ds(query_at + u * CH, CH)], start=True, stop=True)
                last.then_inc(scores_ready, 1)

            def weigh(g, tile, stop):
                for j in range(LANES):
                    at = g * P + 32 * j
                    last = nc.tensor.matmul(out_ps[32 * j:32 * j + 32, 0:CH], v_tile[tile][:, at:at + 32],
                                            probs[:, LANES * g + j, :], start=False, stop=stop)
                last.then_inc(pv_done, 1)

            def key_tile(n, here, after, tile, stop=False):
                pe.wait_ge(probs_ready, n * TRIPLES + 1)
                score(2, *here)
                pe.wait_ge(probs_ready, n * TRIPLES + 2)
                score(3, *here)
                pe.wait_ge(v_ready, n + 1)
                weigh(0, tile, False)
                pe.wait_ge(probs_ready, n * TRIPLES + 3)
                score(0, *after)
                weigh(1, tile, False)
                pe.wait_ge(probs_ready, n * TRIPLES + 4)
                score(1, *after)
                weigh(2, tile, stop)

            pe.wait_ge(cleared, CLEARS)
            pe.wait_ge(keys_loaded, 16)
            pe.wait_ge(queries_loaded, Q_DMAS)
            score(0, 0, 0)
            score(1, 0, 0)
            with pe.Fori(0, NCHUNK) as c:
                k_buf, q_buf = (c // CHUNKS % 2) * K_BUF, (c % 2) * Q_BUF
                next_k, next_q = ((c + 1) // CHUNKS % 2) * K_BUF, ((c + 1) % 2) * Q_BUF
                pe.wait_ge(out_evacuated, c + 1)
                nc.tensor.matmul(out_ps[:, 0:CH], zeros[:, 0:P], zeros[:], start=True, stop=False)
                with pe.Fori(0, PAIRS) as i:
                    at = k_buf + i * (2 * P)
                    key_tile(c * KT + i * 2, (at, q_buf), (at + P, q_buf), 0)
                    key_tile(c * KT + i * 2 + 1, (at + P, q_buf), (at + 2 * P, q_buf), 1)
                pe.wait_ge(queries_loaded, c * Q_DMAS + 2 * Q_DMAS)
                pe.wait_ge(keys_loaded, ((c + 1) // CHUNKS) * 16 + 16)
                key_tile(c * KT + KT - 1, (k_buf + (KT - 1) * P, q_buf), (next_k, next_q), 2, stop=True)


def experts_phase(nc, h_s, ot_s, w_combine, den_select, ident, w1, b1, w2, b2, down_w, down_b, up_w, gamma, beta, out):
    CHUNK_D = EXP_D // P
    with ExitStack() as ctx:
        def sb(name, shape, dt=F32):
            return ctx.enter_context(nc.sbuf_tensor(name, shape, dt))

        def ps(name, shape, dt=F32):
            return ctx.enter_context(nc.psum_tensor(name, shape, dt))

        def sem(name):
            return ctx.enter_context(nc.semaphore(name))

        comb = sb("comb", [P, DIM])
        den = sb("den_select_sb", [P, P])
        idf = sb("ident_sb", [P, P])
        w1_sb = sb("w1_sb", [HALF, 2, HALF])
        b1_sb = sb("b1_sb", [HALF, 1])
        w2_sb = sb("w2_sb", [HALF + 1, EXPERTS])
        down = sb("down", [HALF, 2, EXPERTS, EXP_D])
        down_bias = sb("down_bias", [P, EXPERTS * CHUNK_D])
        up = sb("up", [P, EXPERTS * CHUNK_D, DIM])
        gamma_sb = sb("gamma_sb", [P, DIM])
        beta_sb = sb("beta_sb", [P, DIM])

        h_in = [sb(f"h_in{i}", [P, ST, DIM]) for i in range(2)]
        ot = [sb(f"ot{i}", [P, SN]) for i in range(2)]
        rden = sb("rden", [P, SN])
        att = sb("att", [P, SN])
        h2 = [sb(f"h2_{i}", [P, ST, DIM]) for i in range(2)]
        y = [sb(f"y{i}", [P, ST, DIM]) for i in range(2)]
        yt = [sb(f"yt{i}", [HALF, 2, SN]) for i in range(2)]
        hid = sb("hid", [HALF + 1, SN])
        logit = sb("logit", [P, ST, EXPERTS])
        expo = sb("expo", [P, ST, EXPERTS])
        route = sb("route", [P, ST, 2 * EXPERTS])
        top = sb("top", [P, ST, EXPERTS])
        pick = sb("pick", [P, ST, EXPERTS])
        left = sb("left", [P, ST, 2 * EXPERTS])
        gates = [sb(f"gates{i}", [P, ST, EXPERTS]) for i in range(2)]
        s1, s2 = sb("s1", [P, ST]), sb("s2", [P, ST])
        zt = [sb(f"zt{i}", [P, CHUNK_D, SN]) for i in range(2)]
        moe = sb("moe", [P, ST, DIM])
        fin = [sb(f"fin{i}", [P, ST, DIM]) for i in range(2)]
        stats = sb("stats_e", [P, ST, 6])
        mv = sb("mv_e", [P, ST, 2])
        vare, rstd, tmp = (sb(n, [P, ST]) for n in ("vare_e", "rstd_e", "tmp_e"))
        tmpi = sb("tmpi_e", [P, ST], I32)

        z_ps = [ps(f"z_ps{i}", [P, CHUNK_D, 512]) for i in range(2)]
        up_ps = ps("up_ps", [P, 4, 256])
        pre_ps = ps("pre_ps", [P, 2, 512])
        pre_tiles = pre_ps[:].rearrange("p b (t x) -> p (b t) x", x=256)

        consts_loaded = sem("consts_loaded_e")
        cleared = sem("cleared_e")
        loaded = [sem(f"loaded{i}") for i in range(2)]
        pre_mm = sem("pre_mm")
        pre_act = sem("pre_act")
        pre_dve = sem("pre_dve")
        down_done = sem("down_done")
        z_ready = sem("z_ready")
        up_done = sem("up_done")
        added = sem("added")
        fin_ready = sem("fin_ready")
        pool_steps = sem("pool_steps")
        stored = [sem(f"out_stored{i}") for i in range(2)]
        dve_steps = sem("dve_steps_e")
        idle = sem("idle_e")
        ALL_CONSTS = (LANES * GROUPS + 7 + 5) * 16

        block = ctx.enter_context(nc.Block())

        def all_supertiles(eng, prologue, body):
            prologue()
            with eng.Fori(0, NSUPER // 2 - 1) as i:
                body(i * 2, i, 0, True)
                body(i * 2 + 1, i, 1, True)
            body(NSUPER - 2, NSUPER // 2 - 1, 0, True)
            body(NSUPER - 1, NSUPER // 2 - 1, 1, False)

        @block.sync
        def _(sp):
            def const(dst, src):
                sp.dma_start(dst, src).then_inc(consts_loaded, 16)

            sp.wait_ge(cleared, 1)
            for j in range(LANES):
                for g in range(GROUPS):
                    at, row = 32 * j + DK * g, (LANES * g + j) * DK
                    const(comb[at:at + DK, :], w_combine[row:row + DK, :])
            const(den[:], den_select)
            const(idf[:], ident)

            def load(s, par):
                sp.dma_start(ot[par][:], ot_s[:, ds(s * SN, SN)]).then_inc(loaded[par], 16)
                sp.dma_start(h_in[par][:], h_s[ds(s * SN, SN), :].rearrange("(t p) d -> p t d", p=P)).then_inc(loaded[par], 16)

            load(0, 0)
            const(w1_sb[:], w1.rearrange("(k p) d -> p k d", k=2))
            for k in range(2):
                const(down[:, k], down_w[:, k * HALF:(k + 1) * HALF, :].rearrange("e p d -> p e d"))
            load(1, 1)
            const(up[:], up_w.rearrange("e (c p) h -> p (e c) h", c=CHUNK_D))
            const(gamma_sb[:], gamma.partition_broadcast(P))

            def load_and_store(s, i, par, more):
                if more:
                    wait_apart(sp, pre_dve, s * 3 + 3, idle)
                    load(s + 2, par)
                wait_apart(sp, pool_steps, s * 3 + 3, idle)
                sp.dma_start(out[ds(s * SN, SN), :].rearrange("(t p) d -> p t d", p=P), fin[par][:]).then_inc(stored[par], 16)

            with sp.Fori(0, NSUPER // 2 - 1) as i:
                load_and_store(i * 2, i, 0, True)
                load_and_store(i * 2 + 1, i, 1, True)
            load_and_store(NSUPER - 2, NSUPER // 2 - 1, 0, False)
            load_and_store(NSUPER - 1, NSUPER // 2 - 1, 1, False)
            for par in range(2):
                sp.wait_ge(stored[par], (NSUPER // 2) * 16 + 16)

        @block.gpsimd
        def _(pool):
            pool.wait_ge(consts_loaded, ALL_CONSTS)

            def finish(s, i, par, _):
                wide = [P, ST, DIM]
                wait_apart(pool, fin_ready, s + 1, idle)
                nc.gpsimd.tensor_tensor(fin[par][:], fin[par][:], gamma_sb[:].unsqueeze(1).broadcast_to(wide),
                                        ALU.mult).then_inc(pool_steps, 1)
                wait_apart(pool, pool_steps, s * 3 + 1, idle)
                nc.gpsimd.tensor_tensor(fin[par][:], fin[par][:], beta_sb[:].unsqueeze(1).broadcast_to(wide),
                                        ALU.add).then_inc(pool_steps, 1)
                wait_apart(pool, pool_steps, s * 3 + 2, idle)
                nc.gpsimd.tensor_tensor(fin[par][:], fin[par][:], h2[par][:], ALU.add).then_inc(pool_steps, 1)

            all_supertiles(pool, lambda: None, finish)

        @block.scalar
        def _(act):
            for dst, src in ((b1_sb[:], b1.rearrange("(p a) -> p a", a=1)), (w2_sb[0:HALF, :], w2),
                             (w2_sb[HALF:HALF + 1, :], b2.rearrange("(a e) -> a e", a=1)),
                             (down_bias[:], down_b),
                             (beta_sb[:], beta.partition_broadcast(P))):
                act.dma_start(dst, src).then_inc(consts_loaded, 16)
            nc.scalar.preload_act_table(ACT.Gelu)
            act.wait_ge(consts_loaded, ALL_CONSTS)

            def copy_yt(s, par):
                act.wait_ge(pre_mm, s * 5 + 3)
                nc.scalar.activation(yt[par][:], pre_ps[0:HALF, :, 0:SN], ACT.Copy).then_inc(pre_act, 1)

            def gate_hidden(s):
                act.wait_ge(pre_mm, s * 5 + 4)
                nc.scalar.activation(hid[0:HALF, :], pre_ps[0:HALF, 0, 0:SN], ACT.Gelu, bias=b1_sb[:, 0:1]).then_inc(pre_act, 1)

            def gate_exp(s):
                act.wait_ge(pre_dve, s * 3 + 4)
                nc.scalar.activation(expo[:], logit[:], ACT.Exp).then_inc(pre_act, 1)

            def prologue():
                copy_yt(0, 0)
                gate_hidden(0)
                gate_exp(0)

            def body(s, i, par, has_next):
                for e in range(EXPERTS):
                    act.wait_ge(down_done, s * EXPERTS + (e + 1))
                    act.wait_ge(up_done, s * EXPERTS + (e + 1))
                    for c in range(CHUNK_D):
                        col = e * CHUNK_D + c
                        last = nc.scalar.activation(zt[e % 2][:, c, :], z_ps[e % 2][:, c, 0:SN], ACT.Gelu,
                                                    bias=down_bias[:, col:col + 1])
                    last.then_inc(z_ready, 1)
                    if has_next and e == 4:
                        copy_yt(s + 1, 1 - par)
                    if has_next and e == 5:
                        gate_hidden(s + 1)
                if has_next:
                    gate_exp(s + 1)

            all_supertiles(act, prologue, body)

        @block.vector
        def _(dve):
            nc.vector.memset(comb[:], 0.0).then_inc(cleared, 1)
            nc.vector.memset(hid[HALF:HALF + 1, :], 1.0).then_inc(cleared, 1)
            do = Steps(dve, dve_steps)
            do(nc.vector.memset(route[:], -1.0))
            do(nc.vector.memset(pick[:], -1.0))
            dve.sem_inc(pre_dve, 1)
            dve.sem_inc(z_ready, 2)
            dve.sem_inc(up_done, 2)
            dve.sem_inc(added, 1)
            dve.sem_inc(stored[0], 16)
            dve.sem_inc(stored[1], 16)

            def attention_out(s, i, par):
                dve.wait_ge(pre_mm, s * 5 + 1)
                do(nc.vector.reciprocal(rden[:], pre_ps[:, 0, 0:SN]))
                do.settle()
                nc.vector.tensor_tensor(att[:], ot[par][:], rden[:], ALU.mult).then_inc(pre_dve, 1)

            def residual_and_norm(s, i, par):
                dve.wait_ge(pre_mm, s * 5 + 2)
                dve.wait_ge(stored[par], i * 16 + 16)
                do(nc.vector.tensor_tensor(h2[par][:], pre_tiles[:, 0:ST, 0:DIM], h_in[par][:], ALU.add))
                layer_stats(nc, do, idle, h2[par], ST, P, stats, mv, vare, rstd, tmp, tmpi)
                for t in range(ST):
                    last = nc.vector.tensor_scalar(y[par][:, t, :], h2[par][:, t, :], mv[:, t, 0:1], rstd[:, t:t + 1],
                                                   ALU.subtract, ALU.mult)
                last.then_inc(pre_dve, 1)

            def gate_logits(s):
                dve.wait_ge(pre_mm, s * 5 + 5)
                lg = pre_ps[:, 1, 0:ST * EXPERTS].rearrange("p (t e) -> p t e", e=EXPERTS)
                do(nc.vector.tensor_reduce(s1[:], lg, AX_X, ALU.max))
                do.settle()
                nc.vector.tensor_tensor(logit[:], lg, s1[:].unsqueeze(2).broadcast_to([P, ST, EXPERTS]),
                                        ALU.subtract).then_inc(pre_dve, 1)

            def gate_top2(s, par):
                wide = [P, ST, EXPERTS]
                dve.wait_ge(pre_act, s * 3 + 3)
                do(nc.vector.tensor_reduce(s1[:], expo[:], AX_X, ALU.add))
                do.settle()
                do(nc.vector.reciprocal(s2[:], s1[:]))
                do.settle()
                do(nc.vector.tensor_tensor(route[:, :, 0:EXPERTS], expo[:], s2[:].unsqueeze(2).broadcast_to(wide), ALU.mult))
                do.settle(idle)
                for t in range(ST):
                    do(nc.vector.max(top[:, t, :], route[:, t, 0:EXPERTS]))
                do.settle()
                do(nc.vector.tensor_copy(pick[:, :, 0:2], top[:, :, 0:2]))
                do.settle(idle)
                for t in range(ST):
                    do(nc.vector.match_replace(left[:, t, :], pick[:, t, :], route[:, t, :], 0.0))
                do.settle()
                do(nc.vector.tensor_tensor(top[:], route[:, :, 0:EXPERTS], left[:, :, 0:EXPERTS], ALU.subtract))
                do.settle()
                do(nc.vector.tensor_reduce(s1[:], top[:], AX_X, ALU.add))
                do.settle()
                do(nc.vector.tensor_scalar(s1[:], s1[:], GATE_EPS, None, ALU.add))
                do.settle()
                do(nc.vector.reciprocal(s2[:], s1[:]))
                do.settle()
                do(nc.vector.tensor_tensor(gates[par][:], top[:], s2[:].unsqueeze(2).broadcast_to(wide), ALU.mult))
                do.settle()

            def prologue():
                dve.wait_ge(loaded[0], 32)
                attention_out(0, 0, 0)
                residual_and_norm(0, 0, 0)
                gate_logits(0)
                gate_top2(0, 0)

            def body(s, i, par, has_next):
                nonlocal do
                do = Steps(dve, dve_steps, prologue_steps + s * SUPER_STEPS)
                nxt = (s + 1, i + par, 1 - par)
                for e in range(EXPERTS):
                    dve.wait_ge(up_done, s * EXPERTS + (e + 3))
                    do.settle()
                    for t in range(ST):
                        so_far = moe[:, t, :] if e else y[par][:, t, :]
                        do(nc.vector.scalar_tensor_tensor(moe[:, t, :], up_ps[:, t, 0:DIM], gates[par][:, t, e:e + 1], so_far,
                                                          ALU.mult, ALU.add))
                    do.settle()
                    dve.sem_inc(added, 1)
                    if has_next and e == 0:
                        dve.wait_ge(loaded[1 - par], (nxt[1] + 1) * 32)
                        attention_out(*nxt)
                    if has_next and e == 1:
                        residual_and_norm(*nxt)
                    if has_next and e == 6:
                        gate_logits(s + 1)
                if has_next:
                    gate_top2(s + 1, 1 - par)
                layer_stats(nc, do, idle, moe, ST, P, stats, mv, vare, rstd, tmp, tmpi)
                dve.wait_ge(stored[par], i * 16 + 16)
                for t in range(ST):
                    do(nc.vector.tensor_scalar(fin[par][:, t, :], moe[:, t, :], mv[:, t, 0:1], rstd[:, t:t + 1],
                                               ALU.subtract, ALU.mult))
                do.settle()
                dve.sem_inc(fin_ready, 1)
                if has_next:
                    assert do.n == SUPER_STEPS, do.n

            LN_STEPS = 2 * ST + 1 + 11
            GATE_STEPS = 3 + ST + 1 + ST + 5
            SUPER_STEPS = EXPERTS * ST + 1 + 1 + LN_STEPS + 1 + GATE_STEPS + LN_STEPS + ST
            prologue_steps = 2 + 1 + 1 + LN_STEPS + 1 + GATE_STEPS
            all_supertiles(dve, prologue, body)

        @block.tensor
        def _(pe):
            pe.wait_ge(consts_loaded, ALL_CONSTS)
            pe.wait_ge(cleared, 2)

            def denominators(s, par):
                pe.wait_ge(pre_dve, s * 3 + 1)
                nc.tensor.matmul(pre_ps[:, 0, 0:SN], den[:], ot[par][:], start=True, stop=True).then_inc(pre_mm, 1)

            def project(s):
                pe.wait_ge(pre_dve, s * 3 + 2)
                for t in range(ST):
                    last = nc.tensor.matmul(pre_tiles[:, t, 0:DIM], att[:, t * P:(t + 1) * P], comb[:], start=True, stop=True)
                last.then_inc(pre_mm, 1)

            def transpose_y(s, par):
                pe.wait_ge(pre_dve, s * 3 + 3)
                for k in range(2):
                    for t in range(ST):
                        last = nc.tensor.transpose(pre_ps[0:HALF, k, t * P:(t + 1) * P],
                                                   y[par][:, t, k * HALF:(k + 1) * HALF], idf[:])
                last.then_inc(pre_mm, 1)

            def gate_hidden(s, par):
                pe.wait_ge(pre_act, s * 3 + 1)
                for k in range(2):
                    last = nc.tensor.matmul(pre_ps[0:HALF, 0, 0:SN], w1_sb[:, k, :], yt[par][:, k, :],
                                            start=(k == 0), stop=(k == 1))
                last.then_inc(pre_mm, 1)

            def gate_logits(s):
                pe.wait_ge(pre_act, s * 3 + 2)
                for t in range(ST):
                    last = nc.tensor.matmul(pre_ps[:, 1, t * EXPERTS:(t + 1) * EXPERTS], hid[:, t * P:(t + 1) * P], w2_sb[:],
                                            start=True, stop=True)
                last.then_inc(pre_mm, 1)

            def go_down(s, par, e):
                pe.wait_ge(z_ready, s * EXPERTS + (e + 1))
                for c in range(CHUNK_D):
                    for k in range(2):
                        last = nc.tensor.matmul(z_ps[e % 2][:, c, 0:SN], down[:, k, e, c * P:(c + 1) * P], yt[par][:, k, :],
                                                start=(k == 0), stop=(k == 1))
                last.then_inc(down_done, 1)

            def go_up(s, e):
                pe.wait_ge(z_ready, s * EXPERTS + (e + 3))
                pe.wait_ge(added, s * EXPERTS + (e + 1))
                for t in range(ST):
                    for c in range(CHUNK_D):
                        last = nc.tensor.matmul(up_ps[:, t, 0:DIM], zt[e % 2][:, c, t * P:(t + 1) * P],
                                                up[:, e * CHUNK_D + c, :], start=(c == 0), stop=(c == CHUNK_D - 1))
                last.then_inc(up_done, 1)

            def prologue():
                pe.wait_ge(loaded[0], 32)
                denominators(0, 0)
                project(0)
                transpose_y(0, 0)
                gate_hidden(0, 0)
                gate_logits(0)

            def body(s, i, par, has_next):
                go_down(s, par, 0)
                for e in range(EXPERTS):
                    if e + 1 < EXPERTS:
                        go_down(s, par, e + 1)
                    go_up(s, e)
                    if has_next and e == 0:
                        pe.wait_ge(loaded[1 - par], (i + par + 1) * 32)
                        denominators(s + 1, 1 - par)
                    if has_next and e == 1:
                        project(s + 1)
                    if has_next and e == 3:
                        transpose_y(s + 1, 1 - par)
                    if has_next and e == 4:
                        gate_hidden(s + 1, 1 - par)
                    if has_next and e == 5:
                        gate_logits(s + 1)

            all_supertiles(pe, prologue, body)


def fusion_kernel(nc, x, txt, tok_w, tok_b, theta, w_combine, w1, b1, w2, b2, down_w, down_b, up_w, gamma, beta,
                  ident, ident16, den_select, out):
    h_s = nc.dram_tensor("h_scratch", (NTOK, DIM), F32).ap()
    q_s = nc.dram_tensor("q_scratch", (NTOK, HALF), F32).ap()
    kt_s = nc.dram_tensor("keys_scratch", (B, P, GROUPS, T), F16).ap()
    qt_s = nc.dram_tensor("queries_scratch", (B, P, GROUPS, T), F16).ap()
    ot_s = nc.dram_tensor("attention_scratch", (P, NTOK), F32).ap()
    tokens_phase(nc, x, txt, tok_w, tok_b, theta, ident16, h_s, q_s, kt_s, qt_s)
    attention_phase(nc, q_s, kt_s, qt_s, ot_s)
    experts_phase(nc, h_s, ot_s, w_combine, den_select, ident, w1, b1, w2, b2, down_w, down_b, up_w, gamma, beta,
                  out.rearrange("b t d -> (b t) d"))


def _denominator_rows():
    select = np.zeros((P, P), np.float32)
    for m in range(P):
        j, r = divmod(m, 32)
        g = r // DK if r < GROUPS * DK else min(r - GROUPS * DK, 0)
        select[32 * j + GROUPS * DK + g, m] = 1.0
    return select


def kernel(**inputs):
    import concourse.bacc as bacc
    from concourse.bass_utils import run_bass_kernel_spmd

    given = {k: np.asarray(v) for k, v in inputs.items()}
    arrays = {
        "x": given["x"],
        "txt": given["txt"],
        "tok_w": np.ascontiguousarray(given["L0_tok_W"].reshape(DIM, C_IN, 3, 3).transpose(2, 3, 1, 0)),
        "tok_b": given["L0_tok_b"],
        "theta": given["L0_attn_theta"],
        "w_combine": np.ascontiguousarray(given["L0_attn_W_combine"].T),
        "w1": given["L0_ffn_w1"],
        "b1": given["L0_ffn_b1"],
        "w2": given["L0_ffn_w2"],
        "b2": given["L0_ffn_b2"],
        "down_w": given["L0_ffn_down_w"],
        "down_b": np.ascontiguousarray(given["L0_ffn_down_b"].reshape(-1, P).T),
        "up_w": given["L0_ffn_up_w"],
        "gamma": given["L0_ffn_gamma"],
        "beta": given["L0_ffn_beta"],
        "ident": np.eye(P, dtype=np.float32),
        "ident16": np.eye(P, dtype=np.float16),
        "den_select": _denominator_rows(),
    }
    nc = bacc.Bacc("TRN2", target_bir_lowering=False, num_devices=1)
    in_maps, args = {}, []
    for name, a in arrays.items():
        in_maps[f"in_{name}"] = a
        args.append(nc.dram_tensor(f"in_{name}", a.shape, mybir.dt.from_np(a.dtype), kind="ExternalInput").ap())
    args.append(nc.dram_tensor("out_0", (B, T, DIM), F32, kind="ExternalOutput").ap())
    fusion_kernel(nc, *args)
    r = run_bass_kernel_spmd(nc, [in_maps], core_ids=[0])
    return r.results[0]["out_0"]
```

```python
import math
from contextlib import ExitStack

import numpy as np
import concourse.bass as bass
from concourse import mybir

F32 = mybir.dt.float32
F16 = mybir.dt.float16
I32 = mybir.dt.int32
ALU = mybir.AluOpType
ACT = mybir.ActivationFunctionType
AX_X = mybir.AxisListType.X
ds = bass.ds

P = 128
B, C_IN, HW = 4, 64, 112
DIM = 192
HALF = DIM // 2
SIDE = HW // 2
IMG = SIDE * SIDE
TXT = 512
T = IMG + TXT
NTOK = B * T
HEADS, DK = 12, 8
GROUPS, LANES = 3, 4
EXPERTS, EXP_D = 8, 256
Q_SCALE = 16.0
LN_EPS = 1e-5
GATE_EPS = 1e-8
RSQRT_MAGIC = float(0x5F3759DF)
ROUND_MAGIC = 1.5 * 2.0 ** 23
TWO_PI_HI = 6.28125
TWO_PI_LO = 2 * math.pi - TWO_PI_HI

BANDS = 7
UNITS = BANDS + 1
TILES = 4
RING = 4
TILE_IMG = 2 * SIDE
BAND_TOK = TILES * TILE_IMG
BAND_ROWS = 16
XROWS = BAND_ROWS // 2 + 1

CH = 456
CHUNKS = T // CH
NCHUNK = B * CHUNKS
KT = -(-T // P)
LAST_KEYS = T - (KT - 1) * P
T_PAD = KT * P
PAIRS = (KT - 1) // 2
PAIR = 2
VROW = LANES * 32 + DK

ST = 3
SN = ST * P
NSUPER = NTOK // SN


def wait_apart(engine, sem, value, idle):
    engine.wait_ge(sem, value)
    engine.sem_inc(idle, 1)


class Steps:

    def __init__(self, engine, sem, base=0):
        self.engine, self.sem, self.base, self.n = engine, sem, base, 0

    def __call__(self, ins):
        ins.then_inc(self.sem, 1)
        self.n += 1
        return ins

    def settle(self, idle=None):
        if idle is None:
            self.engine.wait_ge(self.sem, self.base + self.n)
        else:
            wait_apart(self.engine, self.sem, self.base + self.n, idle)


def newton_rsqrt(nc, do, y, x, t, ti):
    do.settle()
    do(nc.vector.tensor_scalar(ti, x.bitcast(I32), 1, None, ALU.logical_shift_right))
    do.settle()
    do(nc.vector.tensor_scalar(y.bitcast(I32), ti, -1.0, RSQRT_MAGIC, ALU.mult, ALU.add))
    for _ in range(3):
        do.settle()
        do(nc.vector.scalar_tensor_tensor(t, y, -0.5, y, ALU.mult, ALU.mult))
        do.settle()
        do(nc.vector.tensor_tensor(t, t, x, ALU.mult))
        do.settle()
        do(nc.vector.scalar_tensor_tensor(y, t, 1.5, y, ALU.add, ALU.mult))


def layer_stats(nc, do, idle, src, n, rows, stats, mv, vare, rstd, tmp, tmpi):
    do.settle()
    for i in range(n):
        do(nc.vector.bn_stats(stats[0:rows, i, :], src[0:rows, i, :]))
    do.settle(idle)
    for i in range(n):
        do(nc.vector.bn_aggr(mv[0:rows, i, :], stats[0:rows, i, :]))
    do.settle()
    do(nc.vector.tensor_scalar(vare[0:rows, 0:n], mv[0:rows, 0:n, 1], LN_EPS, None, ALU.add))
    newton_rsqrt(nc, do, rstd[0:rows, 0:n], vare[0:rows, 0:n], tmp[0:rows, 0:n], tmpi[0:rows, 0:n])
    do.settle()


def cos_argument(nc, do, arg, x, k, r):
    do.settle()
    do(nc.vector.tensor_scalar(k, x, 1.0 / (2 * math.pi), ROUND_MAGIC, ALU.mult, ALU.add))
    do.settle()
    do(nc.vector.tensor_scalar(k, k, ROUND_MAGIC, None, ALU.subtract))
    do.settle()
    do(nc.vector.scalar_tensor_tensor(r, k, -TWO_PI_HI, x, ALU.mult, ALU.add))
    do.settle()
    do(nc.vector.scalar_tensor_tensor(r, k, -TWO_PI_LO, r, ALU.mult, ALU.add))
    do.settle()
    do(nc.vector.scalar_tensor_tensor(arg, r, -1.0, r, ALU.mult, ALU.min))


def tokens_phase(nc, x, txt, tok_w, tok_b, theta, ident16, h_s, q_s, kt_s, qt_s):
    with ExitStack() as ctx:
        def sb(name, shape, dt=F32):
            return ctx.enter_context(nc.sbuf_tensor(name, shape, dt))

        def ps(name, shape, dt=F32):
            return ctx.enter_context(nc.psum_tensor(name, shape, dt))

        def sem(name):
            return ctx.enter_context(nc.semaphore(name))

        xband = {k: sb(f"xband_{k}", [P, XROWS, HW]) for k in ("top", "odd", "even")}
        planes = [sb(f"planes{i}", [P, 3, XROWS, SIDE]) for i in range(2)]
        w01 = sb("w01", [P, 3, DIM])
        w2 = sb("w2_taps", [P, 3, DIM])
        bias = sb("tok_bias", [P, DIM])
        id16 = sb("id16", [P, P], F16)
        theta_sb = sb("theta_sb", [P, HALF])
        cos_theta = sb("cos_theta", [P, HALF])
        half_pi = sb("half_pi", [P, 1])
        h = [sb(f"h{i}", [P, TILES, DIM]) for i in range(RING)]
        h_txt = sb("h_txt", [P, TILES, DIM])
        q = [sb(f"q{i}", [P, TILES, HALF]) for i in range(RING)]
        q_hi = [sb(f"q_hi{i}", [P, TILES, HALF], F16) for i in range(2)]
        q_lo = [sb(f"q_lo{i}", [P, TILES, HALF], F16) for i in range(2)]
        k_form = [sb(f"k_form{i}", [P, TILES, GROUPS * P], F16) for i in range(2)]
        q_form = [sb(f"q_form{i}", [P, TILES, GROUPS * P], F16) for i in range(2)]
        k_out = [sb(f"k_out{i}", [P, GROUPS, TXT], F16) for i in range(RING)]
        q_out = [sb(f"q_out{i}", [P, GROUPS, TXT], F16) for i in range(RING)]
        normed = sb("normed", [P, TILES, HALF])
        rounds = sb("rounds", [P, TILES, HALF])
        rest = sb("rest", [P, TILES, HALF])
        arg = [sb(f"arg{i}", [P, TILES, HALF]) for i in range(2)]
        sine = [sb(f"sine{i}", [P, TILES, HALF]) for i in range(2)]
        stats = sb("stats", [P, TILES, 6])
        mv = sb("mv", [P, TILES, 2])
        vare, rstd, tmp = (sb(n, [P, TILES]) for n in ("vare", "rstd", "tmp"))
        tmpi = sb("tmpi", [P, TILES], I32)
        h_ps = [ps(f"h_ps{i}", [P, TILES, 256]) for i in range(2)]
        k_ps = ps("k_ps", [P, 4, 512], F16)
        q_ps = ps("q_ps", [P, 4, 512], F16)

        consts_loaded = sem("consts_loaded")
        cleared = sem("cleared")
        theta_arg = sem("theta_arg")
        theta_sin = sem("theta_sin")
        x_loaded = {k: sem(f"x_loaded_{k}") for k in xband}
        txt_loaded = sem("txt_loaded")
        planes_pool = sem("planes_pool")
        planes_act = sem("planes_act")
        conv_done = sem("conv_done")
        h_evacuated = sem("h_evacuated")
        h_ready = sem("h_ready")
        arg_ready = sem("arg_ready")
        sine_ready = sem("sine_ready")
        split_ready = sem("split_ready")
        forms_ready = sem("forms_ready")
        transposed = sem("transposed")
        t_evacuated = sem("t_evacuated")
        stored = [sem(f"stored{i}") for i in range(RING)]
        dve_steps = sem("dve_steps")
        idle = sem("idle")

        BAND_DMAS = 32
        UNIT_STORES = 4 * 16
        FORM_STEPS = 4

        def h_of(k):
            return h_txt if k == UNITS - 1 else h[k % RING]

        def place(b, k):
            return (b + 1, k - UNITS) if k >= UNITS else (b, k)

        def all_units(eng, slot):
            slot(0, 0, True)
            slot(0, 1, True)
            with eng.Fori(0, B - 1) as b:
                for k in range(2, UNITS + 2):
                    slot(b, k, True)
            for k in range(2, UNITS + 2):
                slot(B - 1, k, False)

        def rows_of(k):
            return P if k == UNITS - 1 else TILE_IMG

        def buffer_of(k):
            return "top" if k == 0 else ("odd", "even")[(k - 1) % 2]

        def build_plane(eng, copy, built, b, k, kx, wait):
            if wait:
                loads = b if k == 0 else b * 3 + (k - 1) // 2
                wait_apart(eng, x_loaded[buffer_of(k)], loads * BAND_DMAS + BAND_DMAS, idle)
                wait_apart(eng, conv_done, b * BANDS + max(k + 1, 2), idle)
            left = 1 if kx == 0 else 0
            first = 1 if kx == 0 else kx - 1
            copy(planes[k % 2][:, kx, :, left:SIDE],
                 xband[buffer_of(k)][:, :, first:first + 2 * (SIDE - left) - 1:2]).then_inc(built, 1)

        block = ctx.enter_context(nc.Block())

        @block.sync
        def _(sp):
            for kx in range(3):
                for ky, dst in ((0, w01[0:C_IN, kx, :]), (1, w01[C_IN:P, kx, :]), (2, w2[0:C_IN, kx, :])):
                    sp.dma_start(dst, tok_w[ky, kx]).then_inc(consts_loaded, 16)
            sp.dma_start(bias[:], tok_b.partition_broadcast(P)).then_inc(consts_loaded, 16)
            sp.dma_start(theta_sb[:], theta.partition_broadcast(P)).then_inc(consts_loaded, 16)
            sp.dma_start(id16[:], ident16).then_inc(consts_loaded, 16)
            sp.wait_ge(cleared, 6)

            def load_band(b, k, where, built):
                wait_apart(sp, planes_act, b * BANDS + built + 2, idle)
                wait_apart(sp, planes_pool, (b * BANDS + built + 2) * 2, idle)
                rows = x[ds(b, 1)].rearrange("b c (r two) w -> (b c) two r w", two=2)
                above = 1 if where == "top" else 0
                half = BAND_ROWS // 2
                sp.dma_start(xband[where][0:C_IN, above:XROWS, :],
                             rows[:, 1, k * half - 1 + above:(k + 1) * half, :]).then_inc(x_loaded[where], 16)
                sp.dma_start(xband[where][C_IN:P, 0:half, :],
                             rows[:, 0, k * half:(k + 1) * half, :]).then_inc(x_loaded[where], 16)

            with sp.Fori(0, B) as b:
                load_band(b, 0, "top", -1)
                for k in range(1, BANDS):
                    load_band(b, k, buffer_of(k), k - 1 if k > 2 else k - 2)
                    if k == 3:
                        wait_apart(sp, stored[(UNITS - 1) % RING], b * (UNITS // RING * UNIT_STORES) + UNIT_STORES, idle)
                        sp.dma_start(h_txt[:], txt[ds(b, 1)].rearrange("b (t p) d -> p (b t) d", p=P)).then_inc(txt_loaded, 16)

        @block.gpsimd
        def _(pool):
            for k in ("top", "odd", "even"):
                nc.gpsimd.memset(xband[k][:], 0.0).then_inc(cleared, 1)
            for par in range(2):
                nc.gpsimd.memset(planes[par][:, 0, :, 0], 0.0).then_inc(cleared, 1)

            def planes_of(b, k):
                if k < BANDS:
                    for kx in (1, 2):
                        build_plane(pool, nc.gpsimd.tensor_copy, planes_pool, b, k, kx, wait=(kx == 1))

            def slot(b, k, more):
                if k + 1 < UNITS or more:
                    planes_of(*place(b, k + 1))

            planes_of(0, 0)
            all_units(pool, slot)

        @block.scalar
        def _(act):
            nc.scalar.preload_act_table(ACT.Sin)
            act.wait_ge(theta_arg, 1)
            nc.scalar.activation(cos_theta[:], theta_sb[:], ACT.Sin, bias=half_pi[:, 0:1]).then_inc(theta_sin, 1)

            def take_sine(b, k):
                n, par, rows = b * UNITS + k, k % 2, rows_of(k)
                act.wait_ge(arg_ready, n + 1)
                nc.scalar.activation(sine[par][0:rows], arg[par][0:rows], ACT.Sin,
                                     bias=half_pi[0:rows, 0:1]).then_inc(sine_ready, 1)

            def expand(b, k):
                n, par, rows = b * UNITS + k, k % 2, rows_of(k)
                act.wait_ge(split_ready, n + 1)
                act.wait_ge(transposed, n + 1)
                hi = q_hi[par][0:rows].rearrange("p t (h d) -> p (t h) d", d=DK).unsqueeze(2)
                lo = q_lo[par][0:rows].rearrange("p t (h d) -> p (t h) d", d=DK).unsqueeze(2)
                both = [rows, TILES * HEADS, 2, DK]
                kf = k_form[par][0:rows].rearrange("p t (h r d) -> p (t h) r d", r=4, d=DK)
                qf = q_form[par][0:rows].rearrange("p t (h r d) -> p (t h) r d", r=4, d=DK)
                for dst, src in ((kf[:, :, 0:2, :], hi), (kf[:, :, 2:4, :], lo), (qf[:, :, 0:4:2, :], hi), (qf[:, :, 1:4:2, :], lo)):
                    nc.scalar.activation(dst, src.broadcast_to(both), ACT.Copy).then_inc(forms_ready, 1)

            def evacuate(b, k):
                n, par, rows = b * UNITS + k, k % 2, rows_of(k)
                tok = TILES * rows
                act.wait_ge(transposed, n + 3)
                act.wait_ge(stored[k % RING], (b * (UNITS // RING) + k // RING) * UNIT_STORES + UNIT_STORES)
                nc.scalar.activation(k_out[k % RING][:, :, 0:tok], k_ps[:, 0:GROUPS, 0:tok], ACT.Copy).then_inc(t_evacuated, 1)
                nc.scalar.activation(q_out[k % RING][:, :, 0:tok], q_ps[:, 0:GROUPS, 0:tok], ACT.Copy).then_inc(t_evacuated, 1)
                act.wait_ge(t_evacuated, n * 2 + 4)
                at = k * BAND_TOK
                for src, dst in ((k_out, kt_s), (q_out, qt_s)):
                    act.dma_start(dst[ds(b, 1), :, :, at:at + tok].rearrange("b p g t -> (b p) g t"),
                                  src[k % RING][:, :, 0:tok]).then_inc(stored[k % RING], 16)
                act.wait_ge(split_ready, n + 1)
                for src, dst in ((h_of(k), h_s), (q[k % RING], q_s)):
                    act.dma_start(dst[ds(b * T + at, tok), :].rearrange("(t p) d -> p t d", p=rows),
                                  src[0:rows]).then_inc(stored[k % RING], 16)

            def plane_of(b, k):
                if k < BANDS:
                    build_plane(act, nc.scalar.copy, planes_act, b, k, 0, wait=True)

            def slot(b, k, more):
                if k + 1 < UNITS or more:
                    plane_of(*place(b, k + 1))
                if k >= 2:
                    evacuate(b, k - 2)
                if k < UNITS or more:
                    take_sine(*place(b, k))
                if k >= 1 and (k - 1 < UNITS or more):
                    expand(*place(b, k - 1))

            plane_of(0, 0)
            all_units(act, slot)
            for r in range(RING):
                act.wait_ge(stored[r], (B * UNITS // RING + 1) * UNIT_STORES)

        @block.vector
        def _(dve):
            pre = Steps(dve, dve_steps)
            nc.vector.memset(w2[C_IN:P, :, :], 0.0).then_inc(cleared, 1)
            pre(nc.vector.memset(half_pi[:], math.pi / 2))
            dve.wait_ge(consts_loaded, 12 * 16)
            flat = (rounds[:, 0, :], rest[:, 0, :])
            cos_argument(nc, pre, theta_sb[:], theta_sb[:], *flat)
            pre.settle()
            dve.sem_inc(planes_act, 2)
            dve.sem_inc(planes_pool, 4)
            dve.sem_inc(conv_done, 2)
            dve.sem_inc(h_evacuated, 2)
            dve.sem_inc(t_evacuated, 2)
            dve.sem_inc(transposed, 2)
            dve.sem_inc(forms_ready, 2 * FORM_STEPS)
            for r in range(RING):
                dve.sem_inc(stored[r], UNIT_STORES)
            dve.sem_inc(theta_arg, 1)
            dve.wait_ge(theta_sin, 1)
            pre(nc.vector.tensor_scalar(cos_theta[:], cos_theta[:], Q_SCALE, None, ALU.mult))

            def front(b, k, do):
                n, par, rows = b * UNITS + k, k % 2, rows_of(k)
                dve.wait_ge(stored[k % RING], (b * (UNITS // RING) + k // RING) * UNIT_STORES + UNIT_STORES)
                if k < BANDS:
                    dve.wait_ge(conv_done, b * BANDS + k + 3)
                    ins = nc.vector.tensor_tensor(h_of(k)[0:rows], h_ps[k % 2][0:rows, :, 0:DIM],
                                                  bias[0:rows].unsqueeze(1).broadcast_to([rows, TILES, DIM]), ALU.add)
                    ins.then_inc(h_evacuated, 1)
                    dve.wait_ge(h_evacuated, b * BANDS + k + 3)
                else:
                    dve.wait_ge(txt_loaded, b * 16 + 16)
                layer_stats(nc, do, idle, h_of(k), TILES, rows, stats, mv, vare, rstd, tmp, tmpi)
                for t in range(TILES):
                    do(nc.vector.tensor_scalar(normed[0:rows, t, :], h_of(k)[0:rows, t, 0:HALF], mv[0:rows, t, 0:1],
                                               rstd[0:rows, t:t + 1], ALU.subtract, ALU.mult))
                cos_argument(nc, do, arg[par][0:rows], normed[0:rows], rounds[0:rows], rest[0:rows])
                do.settle()
                dve.sem_inc(arg_ready, 1)

            def back(b, k, do):
                n, par, rows = b * UNITS + k, k % 2, rows_of(k)
                dve.wait_ge(sine_ready, n + 1)
                do(nc.vector.tensor_tensor(q[k % RING][0:rows], sine[par][0:rows],
                                           cos_theta[0:rows].unsqueeze(1).broadcast_to([rows, TILES, HALF]), ALU.mult))
                do.settle()
                dve.wait_ge(forms_ready, n * FORM_STEPS + FORM_STEPS)
                do(nc.vector.tensor_copy(q_hi[par][0:rows], q[k % RING][0:rows]))
                do.settle()
                do(nc.vector.tensor_tensor(q_lo[par][0:rows], q[k % RING][0:rows], q_hi[par][0:rows], ALU.subtract))
                do.settle()
                dve.sem_inc(split_ready, 1)

            UNIT_STEPS = 3 * TILES + 1 + 11 + 5 + 3
            BACK_STEPS = 3
            FRONT_STEPS = UNIT_STEPS - BACK_STEPS
            before_2 = pre.n + 2 * FRONT_STEPS + BACK_STEPS

            def slot(b, k, more):
                if k < 2:
                    do = Steps(dve, dve_steps, pre.n + k * FRONT_STEPS)
                else:
                    do = Steps(dve, dve_steps, b * (UNITS * UNIT_STEPS) + before_2 + (k - 2) * UNIT_STEPS)
                if k < UNITS or more:
                    front(*place(b, k), do)
                if k == UNITS and not more:
                    do = Steps(dve, dve_steps, (B * UNITS - 1) * UNIT_STEPS + pre.n + FRONT_STEPS)
                if k >= 1 and (k - 1 < UNITS or more):
                    back(*place(b, k - 1), do)

            all_units(dve, slot)

        @block.tensor
        def _(pe):
            pe.wait_ge(consts_loaded, 12 * 16)
            pe.wait_ge(cleared, 6)

            def convolve(b, k):
                pe.wait_ge(planes_act, b * BANDS + k + 3)
                pe.wait_ge(planes_pool, (b * BANDS + k + 3) * 2)
                pe.wait_ge(h_evacuated, b * BANDS + max(k + 1, 2))
                for t in range(TILES):
                    for m in range(6):
                        oy, kx, w = m // 3, m % 3, (w01, w2)[m // 3]
                        at = (2 * t + oy) * SIDE
                        plane = planes[k % 2][:, kx].rearrange("p r c -> p (r c)")
                        last = nc.tensor.matmul(h_ps[k % 2][0:TILE_IMG, t, 0:DIM], plane[:, at:at + TILE_IMG], w[:, kx, :],
                                                start=(m == 0), stop=(m == 5))
                last.then_inc(conv_done, 1)

            def transpose(b, k):
                n, par, rows = b * UNITS + k, k % 2, rows_of(k)
                pe.wait_ge(forms_ready, (n + 3) * FORM_STEPS)
                pe.wait_ge(t_evacuated, n * 2 + 2)
                for form, out in ((k_form, k_ps), (q_form, q_ps)):
                    for t in range(TILES):
                        for g in range(GROUPS):
                            last = nc.tensor.transpose(out[:, g, t * rows:(t + 1) * rows],
                                                       form[par][0:rows, t, g * P:(g + 1) * P], id16[0:rows, 0:rows])
                last.then_inc(transposed, 1)

            def slot(b, k, more):
                if k < UNITS or more:
                    at = place(b, k)
                    if at[1] < BANDS:
                        convolve(*at)
                if k >= 2:
                    transpose(b, k - 2)

            all_units(pe, slot)


def attention_phase(nc, q_s, kt_s, qt_s, ot_s):
    UNITS_T = GROUPS * LANES
    HEAD_PAIRS = UNITS_T // PAIR
    SCORE_BUFS = 3
    E_SCALE = 1.0 / (Q_SCALE * Q_SCALE * math.sqrt(DK))
    K_BUF, Q_BUF, V_BUF = GROUPS * T_PAD, UNITS_T * CH, KT * HALF
    with ExitStack() as ctx:
        def sb(name, shape, dt=F32):
            return ctx.enter_context(nc.sbuf_tensor(name, shape, dt))

        def ps(name, shape, dt=F32):
            return ctx.enter_context(nc.psum_tensor(name, shape, dt))

        def sem(name):
            return ctx.enter_context(nc.semaphore(name))

        keys = sb("keys", [P, 2 * K_BUF], F16)
        queries = sb("queries", [P, 2 * Q_BUF], F16)
        values = sb("values", [P, 2 * V_BUF])
        v_tile = [sb(f"v_tile{i}", [P, GROUPS * VROW]) for i in range(3)]
        probs = sb("probs", [P, UNITS_T, CH])
        out_sb = sb("out_sb", [P, 2 * CH])
        zeros = sb("zeros", [P, CH], F16)
        scores = [ps(f"scores{i}", [P, PAIR, 512]) for i in range(SCORE_BUFS)]
        out_ps = ps("out_ps", [P, 512])

        cleared = sem("att_cleared")
        keys_loaded = sem("keys_loaded")
        values_loaded = sem("values_loaded")
        queries_loaded = sem("queries_loaded")
        scores_ready = sem("scores_ready")
        probs_ready = sem("probs_ready")
        pv_done = sem("pv_done")
        v_ready = sem("v_ready")
        out_evacuated = sem("out_evacuated")
        out_stored = sem("out_stored")
        idle = sem("idle_a")
        AHEAD = 4
        CLEARS = 8
        Q_DMAS = LANES * 16

        block = ctx.enter_context(nc.Block())

        def chunk_done(c):
            return (c + 1) * (KT * GROUPS) + AHEAD

        @block.sync
        def _(sp):
            sp.wait_ge(cleared, CLEARS)

            def load_batch(b):
                par = b % 2
                kdst = keys[:, par * K_BUF:(par + 1) * K_BUF].rearrange("p (g t) -> p g t", g=GROUPS)
                sp.dma_start(kdst[:, :, 0:T], kt_s[b]).then_inc(keys_loaded, 16)
                wait_apart(sp, keys_loaded, (b + 1) * 16, idle)
                vdst = values[:, par * V_BUF:(par + 1) * V_BUF].rearrange("p (t d) -> p t d", d=HALF)
                full = (KT - 1) * P
                sp.dma_start(vdst[:, 0:KT - 1, :],
                             q_s[b * T:b * T + full, :].rearrange("(t p) d -> p t d", p=P)).then_inc(values_loaded, 16)
                sp.dma_start(vdst[0:LAST_KEYS, KT - 1, :], q_s[b * T + full:(b + 1) * T, :]).then_inc(values_loaded, 16)
                wait_apart(sp, values_loaded, (b + 1) * 32, idle)

            def load_queries(c):
                buf = (c % 2) * Q_BUF
                for j in range(LANES):
                    lane = slice(32 * j, 32 * j + 32)
                    dst = queries[lane, ds(buf, Q_BUF)].rearrange("p (g j t) -> p g j t", g=GROUPS, j=LANES)[:, :, j, :]
                    src = qt_s[ds(c // CHUNKS, 1), lane].rearrange("b p g t -> (b p) g t")[:, :, ds(c % CHUNKS * CH, CH)]
                    sp.dma_start(dst, src).then_inc(queries_loaded, 16)
                wait_apart(sp, queries_loaded, c * Q_DMAS + Q_DMAS, idle)

            def store_out(c):
                wait_apart(sp, out_evacuated, c + 2, idle)
                sp.dma_start(ot_s[:, ds(c * CH, CH)], out_sb[:, ds(c % 2 * CH, CH)]).then_inc(out_stored, 16)
                wait_apart(sp, out_stored, c * 16 + 48, idle)

            load_batch(0)
            load_queries(0)
            load_queries(1)
            load_batch(1)
            for b in range(B):
                if 1 <= b < B - 1:
                    load_batch(b + 1)
                with sp.Fori(b * CHUNKS + 2, min((b + 1) * CHUNKS + 2, NCHUNK)) as c:
                    wait_apart(sp, pv_done, chunk_done(c - 2), idle)
                    load_queries(c)
                    store_out(c - 2)
            sp.sem_inc(queries_loaded, Q_DMAS)
            sp.sem_inc(keys_loaded, 16)
            store_out(NCHUNK - 2)
            store_out(NCHUNK - 1)

        @block.vector
        def _(dve):
            for buf in (queries, keys, zeros, *v_tile):
                nc.vector.memset(buf[:], 0.0).then_inc(cleared, 1)
            dve.wait_ge(cleared, 6)
            ones = []
            for i, rows in ((0, P), (1, P), (2, LAST_KEYS)):
                for g in range(GROUPS):
                    strips = v_tile[i][0:rows, g * P:(g + 1) * P].rearrange("p (j x) -> p j x", x=32)
                    ones.append(nc.vector.memset(strips[:, :, 3 * DK + g], Q_SCALE))
            ones[-2].then_inc(cleared, 1)
            ones[-1].then_inc(cleared, 1)
            dve.sem_inc(out_evacuated, 1)
            dve.sem_inc(out_stored, 32)
            dve.sem_inc(pv_done, AHEAD)
            with dve.Fori(0, NCHUNK) as c:
                dve.wait_ge(pv_done, chunk_done(c))
                dve.wait_ge(out_stored, c * 16 + 16)
                nc.vector.tensor_copy(out_sb[:, ds(c % 2 * CH, CH)], out_ps[:, 0:CH]).then_inc(out_evacuated, 1)

        @block.gpsimd
        def _(pool):
            pool.wait_ge(cleared, CLEARS)

            def place_values(n, tile, rows, start):
                wait_apart(pool, pv_done, n * GROUPS + (AHEAD - GROUPS), idle)
                dst = v_tile[tile][0:rows].rearrange("p (g r) -> p g r", r=VROW)[:, :, 0:P]
                dst = dst.rearrange("p g (j x) -> p g j x", x=32)[:, :, :, 0:DK]
                src = values[0:rows, ds(start, HALF)].rearrange("p (g j d) -> p g j d", g=GROUPS, j=LANES)
                nc.gpsimd.tensor_copy(dst, src).then_inc(v_ready, 1)

            with pool.Fori(0, NCHUNK) as c:
                buf = (c // CHUNKS % 2) * V_BUF
                wait_apart(pool, values_loaded, (c // CHUNKS) * 32 + 32, idle)
                with pool.Fori(0, PAIRS) as i:
                    for x in range(2):
                        place_values(c * KT + i * 2 + x, x, P, buf + i * (2 * HALF) + x * HALF)
                place_values(c * KT + KT - 1, 2, LAST_KEYS, buf + (KT - 1) * HALF)

        @block.scalar
        def _(act):
            nc.scalar.preload_act_table(ACT.Exp)

            def exps(n):
                for k in range(HEAD_PAIRS):
                    act.wait_ge(scores_ready, n * HEAD_PAIRS + (k + 1))
                    act.wait_ge(pv_done, n * GROUPS + (PAIR * k // LANES + 1 + AHEAD - GROUPS))
                    nc.scalar.activation(probs[:, PAIR * k:PAIR * (k + 1), :], scores[k % SCORE_BUFS][:, :, 0:CH],
                                         ACT.Exp, scale=E_SCALE).then_inc(probs_ready, 1)

            with act.Fori(0, NCHUNK) as c:
                with act.Fori(0, PAIRS) as i:
                    exps(c * KT + i * 2)
                    exps(c * KT + i * 2 + 1)
                exps(c * KT + KT - 1)

        @block.tensor
        def _(pe):
            def score(k, key_at, query_at):
                for m in range(PAIR):
                    u = PAIR * k + m
                    last = nc.tensor.matmul(scores[k % SCORE_BUFS][:, m, 0:CH], keys[:, ds(key_at + (u // LANES) * T_PAD, P)],
                                            queries[:, ds(query_at + u * CH, CH)], start=True, stop=True)
                last.then_inc(scores_ready, 1)

            def weigh(g, tile, stop):
                for j in range(LANES):
                    at = g * P + 32 * j
                    last = nc.tensor.matmul(out_ps[32 * j:32 * j + 32, 0:CH], v_tile[tile][:, at:at + 32],
                                            probs[:, LANES * g + j, :], start=False, stop=stop)
                last.then_inc(pv_done, 1)

            def key_tile(n, here, after, tile, stop=False):
                for g in range(GROUPS):
                    for k in (2 * g, 2 * g + 1):
                        pe.wait_ge(probs_ready, n * HEAD_PAIRS + (k + 1))
                        ahead = k + SCORE_BUFS
                        score(ahead % HEAD_PAIRS, *(here if ahead < HEAD_PAIRS else after))
                    if g == 0:
                        pe.wait_ge(v_ready, n + 1)
                    weigh(g, tile, stop and g == GROUPS - 1)

            pe.wait_ge(cleared, CLEARS)
            pe.wait_ge(keys_loaded, 16)
            pe.wait_ge(queries_loaded, Q_DMAS)
            for k in range(SCORE_BUFS):
                score(k, 0, 0)
            with pe.Fori(0, NCHUNK) as c:
                k_buf, q_buf = (c // CHUNKS % 2) * K_BUF, (c % 2) * Q_BUF
                next_k, next_q = ((c + 1) // CHUNKS % 2) * K_BUF, ((c + 1) % 2) * Q_BUF
                pe.wait_ge(out_evacuated, c + 1)
                nc.tensor.matmul(out_ps[:, 0:CH], zeros[:, 0:P], zeros[:], start=True, stop=False)
                with pe.Fori(0, PAIRS) as i:
                    at = k_buf + i * (2 * P)
                    key_tile(c * KT + i * 2, (at, q_buf), (at + P, q_buf), 0)
                    key_tile(c * KT + i * 2 + 1, (at + P, q_buf), (at + 2 * P, q_buf), 1)
                pe.wait_ge(queries_loaded, c * Q_DMAS + 2 * Q_DMAS)
                pe.wait_ge(keys_loaded, ((c + 1) // CHUNKS) * 16 + 16)
                key_tile(c * KT + KT - 1, (k_buf + (KT - 1) * P, q_buf), (next_k, next_q), 2, stop=True)


def experts_phase(nc, h_s, ot_s, w_combine, den_select, ident, w1, b1, w2, b2, down_w, down_b, up_w, gamma, beta, out):
    CHUNK_D = EXP_D // P
    with ExitStack() as ctx:
        def sb(name, shape, dt=F32):
            return ctx.enter_context(nc.sbuf_tensor(name, shape, dt))

        def ps(name, shape, dt=F32):
            return ctx.enter_context(nc.psum_tensor(name, shape, dt))

        def sem(name):
            return ctx.enter_context(nc.semaphore(name))

        comb = sb("comb", [P, DIM])
        den = sb("den_select_sb", [P, P])
        idf = sb("ident_sb", [P, P])
        w1_sb = sb("w1_sb", [HALF, 2, HALF])
        b1_sb = sb("b1_sb", [HALF, 1])
        w2_sb = sb("w2_sb", [HALF + 1, EXPERTS])
        down = sb("down", [HALF, 2, EXPERTS, EXP_D])
        down_bias = sb("down_bias", [P, EXPERTS * CHUNK_D])
        up = sb("up", [P, EXPERTS * CHUNK_D, DIM])
        gamma_sb = sb("gamma_sb", [P, DIM])
        beta_sb = sb("beta_sb", [P, DIM])

        h_in = [sb(f"h_in{i}", [P, ST, DIM]) for i in range(2)]
        ot = [sb(f"ot{i}", [P, SN]) for i in range(2)]
        rden = sb("rden", [P, SN])
        att = sb("att", [P, SN])
        h2 = [sb(f"h2_{i}", [P, ST, DIM]) for i in range(2)]
        y = [sb(f"y{i}", [P, ST, DIM]) for i in range(2)]
        yt = [sb(f"yt{i}", [HALF, 2, SN]) for i in range(2)]
        hid = sb("hid", [HALF + 1, SN])
        logit = sb("logit", [P, ST, EXPERTS])
        expo = sb("expo", [P, ST, EXPERTS])
        route = sb("route", [P, ST, 2 * EXPERTS])
        top = sb("top", [P, ST, EXPERTS])
        pick = sb("pick", [P, ST, EXPERTS])
        left = sb("left", [P, ST, 2 * EXPERTS])
        gates = [sb(f"gates{i}", [P, ST, EXPERTS]) for i in range(2)]
        s1, s2 = sb("s1", [P, ST]), sb("s2", [P, ST])
        zt = [sb(f"zt{i}", [P, CHUNK_D, SN]) for i in range(2)]
        moe = sb("moe", [P, ST, DIM])
        fin = [sb(f"fin{i}", [P, ST, DIM]) for i in range(2)]
        stats = sb("stats_e", [P, ST, 6])
        mv = sb("mv_e", [P, ST, 2])
        vare, rstd, tmp = (sb(n, [P, ST]) for n in ("vare_e", "rstd_e", "tmp_e"))
        tmpi = sb("tmpi_e", [P, ST], I32)

        z_ps = [ps(f"z_ps{i}", [P, CHUNK_D, 512]) for i in range(2)]
        up_ps = ps("up_ps", [P, 4, 256])
        pre_ps = ps("pre_ps", [P, 2, 512])
        pre_tiles = pre_ps[:].rearrange("p b (t x) -> p (b t) x", x=256)

        consts_loaded = sem("consts_loaded_e")
        cleared = sem("cleared_e")
        loaded = [sem(f"loaded{i}") for i in range(2)]
        pre_mm = sem("pre_mm")
        pre_act = sem("pre_act")
        pre_dve = sem("pre_dve")
        down_done = sem("down_done")
        z_ready = sem("z_ready")
        up_done = sem("up_done")
        added = sem("added")
        fin_ready = sem("fin_ready")
        pool_steps = sem("pool_steps")
        stored = [sem(f"out_stored{i}") for i in range(2)]
        dve_steps = sem("dve_steps_e")
        idle = sem("idle_e")
        ALL_CONSTS = (LANES * GROUPS + 7 + 5) * 16

        block = ctx.enter_context(nc.Block())

        def all_supertiles(eng, prologue, body):
            prologue()
            with eng.Fori(0, NSUPER // 2 - 1) as i:
                body(i * 2, i, 0, True)
                body(i * 2 + 1, i, 1, True)
            body(NSUPER - 2, NSUPER // 2 - 1, 0, True)
            body(NSUPER - 1, NSUPER // 2 - 1, 1, False)

        @block.sync
        def _(sp):
            def const(dst, src):
                sp.dma_start(dst, src).then_inc(consts_loaded, 16)

            sp.wait_ge(cleared, 1)
            for j in range(LANES):
                for g in range(GROUPS):
                    at, row = 32 * j + DK * g, (LANES * g + j) * DK
                    const(comb[at:at + DK, :], w_combine[row:row + DK, :])
            const(den[:], den_select)
            const(idf[:], ident)

            def load(s, par):
                sp.dma_start(ot[par][:], ot_s[:, ds(s * SN, SN)]).then_inc(loaded[par], 16)
                sp.dma_start(h_in[par][:], h_s[ds(s * SN, SN), :].rearrange("(t p) d -> p t d", p=P)).then_inc(loaded[par], 16)

            load(0, 0)
            const(w1_sb[:], w1.rearrange("(k p) d -> p k d", k=2))
            for k in range(2):
                const(down[:, k], down_w[:, k * HALF:(k + 1) * HALF, :].rearrange("e p d -> p e d"))
            load(1, 1)
            const(up[:], up_w.rearrange("e (c p) h -> p (e c) h", c=CHUNK_D))
            const(gamma_sb[:], gamma.partition_broadcast(P))

            def load_and_store(s, i, par, more):
                if more:
                    wait_apart(sp, pre_dve, s * 3 + 3, idle)
                    load(s + 2, par)
                wait_apart(sp, pool_steps, s * 3 + 3, idle)
                sp.dma_start(out[ds(s * SN, SN), :].rearrange("(t p) d -> p t d", p=P), fin[par][:]).then_inc(stored[par], 16)

            with sp.Fori(0, NSUPER // 2 - 1) as i:
                load_and_store(i * 2, i, 0, True)
                load_and_store(i * 2 + 1, i, 1, True)
            load_and_store(NSUPER - 2, NSUPER // 2 - 1, 0, False)
            load_and_store(NSUPER - 1, NSUPER // 2 - 1, 1, False)
            for par in range(2):
                sp.wait_ge(stored[par], (NSUPER // 2) * 16 + 16)

        @block.gpsimd
        def _(pool):
            pool.wait_ge(consts_loaded, ALL_CONSTS)

            def finish(s, i, par, _):
                wide = [P, ST, DIM]
                wait_apart(pool, fin_ready, s + 1, idle)
                nc.gpsimd.tensor_tensor(fin[par][:], fin[par][:], gamma_sb[:].unsqueeze(1).broadcast_to(wide),
                                        ALU.mult).then_inc(pool_steps, 1)
                wait_apart(pool, pool_steps, s * 3 + 1, idle)
                nc.gpsimd.tensor_tensor(fin[par][:], fin[par][:], beta_sb[:].unsqueeze(1).broadcast_to(wide),
                                        ALU.add).then_inc(pool_steps, 1)
                wait_apart(pool, pool_steps, s * 3 + 2, idle)
                nc.gpsimd.tensor_tensor(fin[par][:], fin[par][:], h2[par][:], ALU.add).then_inc(pool_steps, 1)

            all_supertiles(pool, lambda: None, finish)

        @block.scalar
        def _(act):
            for dst, src in ((b1_sb[:], b1.rearrange("(p a) -> p a", a=1)), (w2_sb[0:HALF, :], w2),
                             (w2_sb[HALF:HALF + 1, :], b2.rearrange("(a e) -> a e", a=1)),
                             (down_bias[:], down_b),
                             (beta_sb[:], beta.partition_broadcast(P))):
                act.dma_start(dst, src).then_inc(consts_loaded, 16)
            nc.scalar.preload_act_table(ACT.Gelu)
            act.wait_ge(consts_loaded, ALL_CONSTS)

            def copy_yt(s, par):
                act.wait_ge(pre_mm, s * 5 + 3)
                nc.scalar.activation(yt[par][:], pre_ps[0:HALF, :, 0:SN], ACT.Copy).then_inc(pre_act, 1)

            def gate_hidden(s):
                act.wait_ge(pre_mm, s * 5 + 4)
                nc.scalar.activation(hid[0:HALF, :], pre_ps[0:HALF, 0, 0:SN], ACT.Gelu, bias=b1_sb[:, 0:1]).then_inc(pre_act, 1)

            def gate_exp(s):
                act.wait_ge(pre_dve, s * 3 + 4)
                nc.scalar.activation(expo[:], logit[:], ACT.Exp).then_inc(pre_act, 1)

            def prologue():
                copy_yt(0, 0)
                gate_hidden(0)
                gate_exp(0)

            def body(s, i, par, has_next):
                for e in range(EXPERTS):
                    act.wait_ge(down_done, s * EXPERTS + (e + 1))
                    act.wait_ge(up_done, s * EXPERTS + (e + 1))
                    for c in range(CHUNK_D):
                        col = e * CHUNK_D + c
                        last = nc.scalar.activation(zt[e % 2][:, c, :], z_ps[e % 2][:, c, 0:SN], ACT.Gelu,
                                                    bias=down_bias[:, col:col + 1])
                    last.then_inc(z_ready, 1)
                    if has_next and e == 4:
                        copy_yt(s + 1, 1 - par)
                    if has_next and e == 5:
                        gate_hidden(s + 1)
                if has_next:
                    gate_exp(s + 1)

            all_supertiles(act, prologue, body)

        @block.vector
        def _(dve):
            nc.vector.memset(comb[:], 0.0).then_inc(cleared, 1)
            nc.vector.memset(hid[HALF:HALF + 1, :], 1.0).then_inc(cleared, 1)
            do = Steps(dve, dve_steps)
            do(nc.vector.memset(route[:], -1.0))
            do(nc.vector.memset(pick[:], -1.0))
            dve.sem_inc(pre_dve, 1)
            dve.sem_inc(z_ready, 2)
            dve.sem_inc(up_done, 2)
            dve.sem_inc(added, 1)
            dve.sem_inc(stored[0], 16)
            dve.sem_inc(stored[1], 16)

            def attention_out(s, i, par):
                dve.wait_ge(pre_mm, s * 5 + 1)
                do(nc.vector.reciprocal(rden[:], pre_ps[:, 0, 0:SN]))
                do.settle()
                nc.vector.tensor_tensor(att[:], ot[par][:], rden[:], ALU.mult).then_inc(pre_dve, 1)

            def residual_and_norm(s, i, par):
                dve.wait_ge(pre_mm, s * 5 + 2)
                dve.wait_ge(stored[par], i * 16 + 16)
                do(nc.vector.tensor_tensor(h2[par][:], pre_tiles[:, 0:ST, 0:DIM], h_in[par][:], ALU.add))
                layer_stats(nc, do, idle, h2[par], ST, P, stats, mv, vare, rstd, tmp, tmpi)
                for t in range(ST):
                    last = nc.vector.tensor_scalar(y[par][:, t, :], h2[par][:, t, :], mv[:, t, 0:1], rstd[:, t:t + 1],
                                                   ALU.subtract, ALU.mult)
                last.then_inc(pre_dve, 1)

            def gate_logits(s):
                dve.wait_ge(pre_mm, s * 5 + 5)
                lg = pre_ps[:, 1, 0:ST * EXPERTS].rearrange("p (t e) -> p t e", e=EXPERTS)
                do(nc.vector.tensor_reduce(s1[:], lg, AX_X, ALU.max))
                do.settle()
                nc.vector.tensor_tensor(logit[:], lg, s1[:].unsqueeze(2).broadcast_to([P, ST, EXPERTS]),
                                        ALU.subtract).then_inc(pre_dve, 1)

            def gate_top2(s, par):
                wide = [P, ST, EXPERTS]
                dve.wait_ge(pre_act, s * 3 + 3)
                do(nc.vector.tensor_reduce(s1[:], expo[:], AX_X, ALU.add))
                do.settle()
                do(nc.vector.reciprocal(s2[:], s1[:]))
                do.settle()
                do(nc.vector.tensor_tensor(route[:, :, 0:EXPERTS], expo[:], s2[:].unsqueeze(2).broadcast_to(wide), ALU.mult))
                do.settle(idle)
                for t in range(ST):
                    do(nc.vector.max(top[:, t, :], route[:, t, 0:EXPERTS]))
                do.settle()
                do(nc.vector.tensor_copy(pick[:, :, 0:2], top[:, :, 0:2]))
                do.settle(idle)
                for t in range(ST):
                    do(nc.vector.match_replace(left[:, t, :], pick[:, t, :], route[:, t, :], 0.0))
                do.settle()
                do(nc.vector.tensor_tensor(top[:], route[:, :, 0:EXPERTS], left[:, :, 0:EXPERTS], ALU.subtract))
                do.settle()
                do(nc.vector.tensor_reduce(s1[:], top[:], AX_X, ALU.add))
                do.settle()
                do(nc.vector.tensor_scalar(s1[:], s1[:], GATE_EPS, None, ALU.add))
                do.settle()
                do(nc.vector.reciprocal(s2[:], s1[:]))
                do.settle()
                do(nc.vector.tensor_tensor(gates[par][:], top[:], s2[:].unsqueeze(2).broadcast_to(wide), ALU.mult))
                do.settle()

            def prologue():
                dve.wait_ge(loaded[0], 32)
                attention_out(0, 0, 0)
                residual_and_norm(0, 0, 0)
                gate_logits(0)
                gate_top2(0, 0)

            def body(s, i, par, has_next):
                nonlocal do
                do = Steps(dve, dve_steps, prologue_steps + s * SUPER_STEPS)
                nxt = (s + 1, i + par, 1 - par)
                for e in range(EXPERTS):
                    dve.wait_ge(up_done, s * EXPERTS + (e + 3))
                    do.settle()
                    for t in range(ST):
                        so_far = moe[:, t, :] if e else y[par][:, t, :]
                        do(nc.vector.scalar_tensor_tensor(moe[:, t, :], up_ps[:, t, 0:DIM], gates[par][:, t, e:e + 1], so_far,
                                                          ALU.mult, ALU.add))
                    do.settle()
                    dve.sem_inc(added, 1)
                    if has_next and e == 0:
                        dve.wait_ge(loaded[1 - par], (nxt[1] + 1) * 32)
                        attention_out(*nxt)
                    if has_next and e == 1:
                        residual_and_norm(*nxt)
                    if has_next and e == 6:
                        gate_logits(s + 1)
                if has_next:
                    gate_top2(s + 1, 1 - par)
                layer_stats(nc, do, idle, moe, ST, P, stats, mv, vare, rstd, tmp, tmpi)
                dve.wait_ge(stored[par], i * 16 + 16)
                for t in range(ST):
                    do(nc.vector.tensor_scalar(fin[par][:, t, :], moe[:, t, :], mv[:, t, 0:1], rstd[:, t:t + 1],
                                               ALU.subtract, ALU.mult))
                do.settle()
                dve.sem_inc(fin_ready, 1)
                if has_next:
                    assert do.n == SUPER_STEPS, do.n

            LN_STEPS = 2 * ST + 1 + 11
            GATE_STEPS = 3 + ST + 1 + ST + 5
            SUPER_STEPS = EXPERTS * ST + 1 + 1 + LN_STEPS + 1 + GATE_STEPS + LN_STEPS + ST
            prologue_steps = 2 + 1 + 1 + LN_STEPS + 1 + GATE_STEPS
            all_supertiles(dve, prologue, body)

        @block.tensor
        def _(pe):
            pe.wait_ge(consts_loaded, ALL_CONSTS)
            pe.wait_ge(cleared, 2)

            def denominators(s, par):
                pe.wait_ge(pre_dve, s * 3 + 1)
                nc.tensor.matmul(pre_ps[:, 0, 0:SN], den[:], ot[par][:], start=True, stop=True).then_inc(pre_mm, 1)

            def project(s):
                pe.wait_ge(pre_dve, s * 3 + 2)
                for t in range(ST):
                    last = nc.tensor.matmul(pre_tiles[:, t, 0:DIM], att[:, t * P:(t + 1) * P], comb[:], start=True, stop=True)
                last.then_inc(pre_mm, 1)

            def transpose_y(s, par):
                pe.wait_ge(pre_dve, s * 3 + 3)
                for k in range(2):
                    for t in range(ST):
                        last = nc.tensor.transpose(pre_ps[0:HALF, k, t * P:(t + 1) * P],
                                                   y[par][:, t, k * HALF:(k + 1) * HALF], idf[:])
                last.then_inc(pre_mm, 1)

            def gate_hidden(s, par):
                pe.wait_ge(pre_act, s * 3 + 1)
                for k in range(2):
                    last = nc.tensor.matmul(pre_ps[0:HALF, 0, 0:SN], w1_sb[:, k, :], yt[par][:, k, :],
                                            start=(k == 0), stop=(k == 1))
                last.then_inc(pre_mm, 1)

            def gate_logits(s):
                pe.wait_ge(pre_act, s * 3 + 2)
                for t in range(ST):
                    last = nc.tensor.matmul(pre_ps[:, 1, t * EXPERTS:(t + 1) * EXPERTS], hid[:, t * P:(t + 1) * P], w2_sb[:],
                                            start=True, stop=True)
                last.then_inc(pre_mm, 1)

            def go_down(s, par, e):
                pe.wait_ge(z_ready, s * EXPERTS + (e + 1))
                for c in range(CHUNK_D):
                    for k in range(2):
                        last = nc.tensor.matmul(z_ps[e % 2][:, c, 0:SN], down[:, k, e, c * P:(c + 1) * P], yt[par][:, k, :],
                                                start=(k == 0), stop=(k == 1))
                last.then_inc(down_done, 1)

            def go_up(s, e):
                pe.wait_ge(z_ready, s * EXPERTS + (e + 3))
                pe.wait_ge(added, s * EXPERTS + (e + 1))
                for t in range(ST):
                    for c in range(CHUNK_D):
                        last = nc.tensor.matmul(up_ps[:, t, 0:DIM], zt[e % 2][:, c, t * P:(t + 1) * P],
                                                up[:, e * CHUNK_D + c, :], start=(c == 0), stop=(c == CHUNK_D - 1))
                last.then_inc(up_done, 1)

            def prologue():
                pe.wait_ge(loaded[0], 32)
                denominators(0, 0)
                project(0)
                transpose_y(0, 0)
                gate_hidden(0, 0)
                gate_logits(0)

            def body(s, i, par, has_next):
                go_down(s, par, 0)
                for e in range(EXPERTS):
                    if e + 1 < EXPERTS:
                        go_down(s, par, e + 1)
                    go_up(s, e)
                    if has_next and e == 0:
                        pe.wait_ge(loaded[1 - par], (i + par + 1) * 32)
                        denominators(s + 1, 1 - par)
                    if has_next and e == 1:
                        project(s + 1)
                    if has_next and e == 3:
                        transpose_y(s + 1, 1 - par)
                    if has_next and e == 4:
                        gate_hidden(s + 1, 1 - par)
                    if has_next and e == 5:
                        gate_logits(s + 1)

            all_supertiles(pe, prologue, body)


def fusion_kernel(nc, x, txt, tok_w, tok_b, theta, w_combine, w1, b1, w2, b2, down_w, down_b, up_w, gamma, beta,
                  ident, ident16, den_select, out):
    h_s = nc.dram_tensor("h_scratch", (NTOK, DIM), F32).ap()
    q_s = nc.dram_tensor("q_scratch", (NTOK, HALF), F32).ap()
    kt_s = nc.dram_tensor("keys_scratch", (B, P, GROUPS, T), F16).ap()
    qt_s = nc.dram_tensor("queries_scratch", (B, P, GROUPS, T), F16).ap()
    ot_s = nc.dram_tensor("attention_scratch", (P, NTOK), F32).ap()
    tokens_phase(nc, x, txt, tok_w, tok_b, theta, ident16, h_s, q_s, kt_s, qt_s)
    attention_phase(nc, q_s, kt_s, qt_s, ot_s)
    experts_phase(nc, h_s, ot_s, w_combine, den_select, ident, w1, b1, w2, b2, down_w, down_b, up_w, gamma, beta,
                  out.rearrange("b t d -> (b t) d"))


def _denominator_rows():
    select = np.zeros((P, P), np.float32)
    for m in range(P):
        j, r = divmod(m, 32)
        g = r // DK if r < GROUPS * DK else min(r - GROUPS * DK, 0)
        select[32 * j + GROUPS * DK + g, m] = 1.0
    return select


def kernel(**inputs):
    import concourse.bacc as bacc
    from concourse.bass_utils import run_bass_kernel_spmd

    given = {k: np.asarray(v) for k, v in inputs.items()}
    arrays = {
        "x": given["x"],
        "txt": given["txt"],
        "tok_w": np.ascontiguousarray(given["L0_tok_W"].reshape(DIM, C_IN, 3, 3).transpose(2, 3, 1, 0)),
        "tok_b": given["L0_tok_b"],
        "theta": given["L0_attn_theta"],
        "w_combine": np.ascontiguousarray(given["L0_attn_W_combine"].T),
        "w1": given["L0_ffn_w1"],
        "b1": given["L0_ffn_b1"],
        "w2": given["L0_ffn_w2"],
        "b2": given["L0_ffn_b2"],
        "down_w": given["L0_ffn_down_w"],
        "down_b": np.ascontiguousarray(given["L0_ffn_down_b"].reshape(-1, P).T),
        "up_w": given["L0_ffn_up_w"],
        "gamma": given["L0_ffn_gamma"],
        "beta": given["L0_ffn_beta"],
        "ident": np.eye(P, dtype=np.float32),
        "ident16": np.eye(P, dtype=np.float16),
        "den_select": _denominator_rows(),
    }
    nc = bacc.Bacc("TRN2", target_bir_lowering=False, num_devices=1)
    in_maps, args = {}, []
    for name, a in arrays.items():
        in_maps[f"in_{name}"] = a
        args.append(nc.dram_tensor(f"in_{name}", a.shape, mybir.dt.from_np(a.dtype), kind="ExternalInput").ap())
    args.append(nc.dram_tensor("out_0", (B, T, DIM), F32, kind="ExternalOutput").ap())
    fusion_kernel(nc, *args)
    r = run_bass_kernel_spmd(nc, [in_maps], core_ids=[0])
    return r.results[0]["out_0"]
```

```python
import math
from contextlib import ExitStack

import numpy as np
import concourse.bass as bass
from concourse import mybir

F32 = mybir.dt.float32
F16 = mybir.dt.float16
I32 = mybir.dt.int32
ALU = mybir.AluOpType
ACT = mybir.ActivationFunctionType
AX_X = mybir.AxisListType.X
ds = bass.ds

P = 128
B, C_IN, HW = 4, 64, 112
DIM = 192
HALF = DIM // 2
SIDE = HW // 2
IMG = SIDE * SIDE
TXT = 512
T = IMG + TXT
NTOK = B * T
HEADS, DK = 12, 8
GROUPS, LANES = 3, 4
EXPERTS, EXP_D = 8, 256
Q_SCALE = 16.0
LN_EPS = 1e-5
GATE_EPS = 1e-8
RSQRT_MAGIC = float(0x5F3759DF)
ROUND_MAGIC = 1.5 * 2.0 ** 23
TWO_PI_HI = 6.28125
TWO_PI_LO = 2 * math.pi - TWO_PI_HI

BANDS = 7
UNITS = BANDS + 1
TILES = 4
RING = 4
TILE_IMG = 2 * SIDE
BAND_TOK = TILES * TILE_IMG
BAND_ROWS = 16
XROWS = BAND_ROWS // 2 + 1

CH = 456
CHUNKS = T // CH
NCHUNK = B * CHUNKS
KT = -(-T // P)
LAST_KEYS = T - (KT - 1) * P
assert LAST_KEYS * 2 == P
PAIRS = (KT - 1) // 2
PAIR = 2
VROW = LANES * 32 + DK

ST = 3
SN = ST * P
NSUPER = NTOK // SN
CHUNK_D = EXP_D // P
GATE_AT = EXPERTS * EXP_D
STACK = GATE_AT + HALF
FORMS = 2 * DIM // P
STACK_ROWS = ((0, 0, 0, P), (1, 0, P, DIM - P), (1, DIM - P, 0, 2 * P - DIM), (2, 0, 2 * P - DIM, P))
Y_SCALE_LOG2 = 4
W_EXPONENT = 13
MAX_SCALE_BITS = 240


def wait_apart(engine, sem, value, idle):
    engine.wait_ge(sem, value)
    engine.sem_inc(idle, 1)


class Steps:

    def __init__(self, engine, sem, base=0):
        self.engine, self.sem, self.base, self.n = engine, sem, base, 0

    def __call__(self, ins):
        ins.then_inc(self.sem, 1)
        self.n += 1
        return ins

    def settle(self, idle=None):
        if idle is None:
            self.engine.wait_ge(self.sem, self.base + self.n)
        else:
            wait_apart(self.engine, self.sem, self.base + self.n, idle)


def newton_rsqrt(nc, do, y, x, t, ti):
    do.settle()
    do(nc.vector.tensor_scalar(ti, x.bitcast(I32), 1, None, ALU.logical_shift_right))
    do.settle()
    do(nc.vector.tensor_scalar(y.bitcast(I32), ti, -1.0, RSQRT_MAGIC, ALU.mult, ALU.add))
    for _ in range(3):
        do.settle()
        do(nc.vector.scalar_tensor_tensor(t, y, -0.5, y, ALU.mult, ALU.mult))
        do.settle()
        do(nc.vector.tensor_tensor(t, t, x, ALU.mult))
        do.settle()
        do(nc.vector.scalar_tensor_tensor(y, t, 1.5, y, ALU.add, ALU.mult))


def row_stats(nc, do, idle, src, n, rows, stats, mv):
    do.settle()
    for i in range(n):
        do(nc.vector.bn_stats(stats[0:rows, i, :], src[0:rows, i, :]))
    do.settle(idle)
    for i in range(n):
        do(nc.vector.bn_aggr(mv[0:rows, i, :], stats[0:rows, i, :]))


def row_rstd(nc, do, n, rows, mv, vare, rstd, tmp, tmpi):
    do.settle()
    do(nc.vector.tensor_scalar(vare[0:rows, 0:n], mv[0:rows, 0:n, 1], LN_EPS, None, ALU.add))
    newton_rsqrt(nc, do, rstd[0:rows, 0:n], vare[0:rows, 0:n], tmp[0:rows, 0:n], tmpi[0:rows, 0:n])
    do.settle()


def cos_argument(nc, do, arg, x, k, r):
    do.settle()
    do(nc.vector.tensor_scalar(k, x, 1.0 / (2 * math.pi), ROUND_MAGIC, ALU.mult, ALU.add))
    do.settle()
    do(nc.vector.tensor_scalar(k, k, ROUND_MAGIC, None, ALU.subtract))
    do.settle()
    do(nc.vector.scalar_tensor_tensor(r, k, -TWO_PI_HI, x, ALU.mult, ALU.add))
    do.settle()
    do(nc.vector.scalar_tensor_tensor(r, k, -TWO_PI_LO, r, ALU.mult, ALU.add))
    do.settle()
    do(nc.vector.scalar_tensor_tensor(arg, r, -1.0, r, ALU.mult, ALU.min))


def tokens_phase(nc, x, txt, tok_w, tok_b, theta, ident16, h_s, q_s, kt_s, qt_s):
    with ExitStack() as ctx:
        def sb(name, shape, dt=F32):
            return ctx.enter_context(nc.sbuf_tensor(name, shape, dt))

        def ps(name, shape, dt=F32):
            return ctx.enter_context(nc.psum_tensor(name, shape, dt))

        def sem(name):
            return ctx.enter_context(nc.semaphore(name))

        xband = {k: sb(f"xband_{k}", [P, XROWS, HW]) for k in ("top", "odd", "even")}
        planes = [sb(f"planes{i}", [P, 3, XROWS, SIDE]) for i in range(2)]
        w01 = sb("w01", [P, 3, DIM])
        w2 = sb("w2_taps", [P, 3, DIM])
        bias = sb("tok_bias", [P, DIM])
        id16 = sb("id16", [P, P], F16)
        theta_sb = sb("theta_sb", [P, HALF])
        cos_theta = sb("cos_theta", [P, HALF])
        half_pi = sb("half_pi", [P, 1])
        h = [sb(f"h{i}", [P, TILES, DIM]) for i in range(RING)]
        h_txt = sb("h_txt", [P, TILES, DIM])
        q = [sb(f"q{i}", [P, TILES, HALF]) for i in range(RING)]
        q_hi = [sb(f"q_hi{i}", [P, TILES, HALF], F16) for i in range(2)]
        q_lo = [sb(f"q_lo{i}", [P, TILES, HALF], F16) for i in range(2)]
        k_form = [sb(f"k_form{i}", [P, TILES, GROUPS * P], F16) for i in range(2)]
        q_form = [sb(f"q_form{i}", [P, TILES, GROUPS * P], F16) for i in range(2)]
        k_out = [sb(f"k_out{i}", [P, GROUPS, TXT], F16) for i in range(RING)]
        q_out = [sb(f"q_out{i}", [P, GROUPS, TXT], F16) for i in range(RING)]
        normed = sb("normed", [P, TILES, HALF])
        rounds = sb("rounds", [P, TILES, HALF])
        rest = sb("rest", [P, TILES, HALF])
        arg = [sb(f"arg{i}", [P, TILES, HALF]) for i in range(2)]
        sine = [sb(f"sine{i}", [P, TILES, HALF]) for i in range(2)]
        stats = sb("stats", [P, TILES, 6])
        mv = sb("mv", [P, TILES, 2])
        vare, rstd, tmp = (sb(n, [P, TILES]) for n in ("vare", "rstd", "tmp"))
        tmpi = sb("tmpi", [P, TILES], I32)
        h_ps = [ps(f"h_ps{i}", [P, TILES, 256]) for i in range(2)]
        k_ps = ps("k_ps", [P, 4, 512], F16)
        q_ps = ps("q_ps", [P, 4, 512], F16)

        consts_loaded = sem("consts_loaded")
        cleared = sem("cleared")
        theta_arg = sem("theta_arg")
        theta_sin = sem("theta_sin")
        x_loaded = {k: sem(f"x_loaded_{k}") for k in xband}
        txt_loaded = sem("txt_loaded")
        planes_pool = sem("planes_pool")
        planes_act = sem("planes_act")
        conv_done = sem("conv_done")
        h_evacuated = sem("h_evacuated")
        h_ready = sem("h_ready")
        arg_ready = sem("arg_ready")
        sine_ready = sem("sine_ready")
        split_ready = sem("split_ready")
        forms_ready = sem("forms_ready")
        transposed = sem("transposed")
        t_evacuated = sem("t_evacuated")
        stored = [sem(f"stored{i}") for i in range(RING)]
        dve_steps = sem("dve_steps")
        idle = sem("idle")

        BAND_DMAS = 32
        UNIT_STORES = 4 * 16
        FORM_STEPS = 4

        def h_of(k):
            return h_txt if k == UNITS - 1 else h[k % RING]

        def place(b, k):
            return (b + 1, k - UNITS) if k >= UNITS else (b, k)

        def all_units(eng, slot):
            slot(0, 0, True)
            slot(0, 1, True)
            with eng.Fori(0, B - 1) as b:
                for k in range(2, UNITS + 2):
                    slot(b, k, True)
            for k in range(2, UNITS + 2):
                slot(B - 1, k, False)

        def rows_of(k):
            return P if k == UNITS - 1 else TILE_IMG

        def buffer_of(k):
            return "top" if k == 0 else ("odd", "even")[(k - 1) % 2]

        def build_plane(eng, copy, built, b, k, kx, wait):
            if wait:
                loads = b if k == 0 else b * 3 + (k - 1) // 2
                wait_apart(eng, x_loaded[buffer_of(k)], loads * BAND_DMAS + BAND_DMAS, idle)
                wait_apart(eng, conv_done, b * BANDS + max(k + 1, 2), idle)
            left = 1 if kx == 0 else 0
            first = 1 if kx == 0 else kx - 1
            copy(planes[k % 2][:, kx, :, left:SIDE],
                 xband[buffer_of(k)][:, :, first:first + 2 * (SIDE - left) - 1:2]).then_inc(built, 1)

        block = ctx.enter_context(nc.Block())

        @block.sync
        def _(sp):
            sp.wait_ge(cleared, 6)

            def load_band(b, k, where, built):
                wait_apart(sp, planes_act, b * BANDS + built + 2, idle)
                wait_apart(sp, planes_pool, (b * BANDS + built + 2) * 2, idle)
                rows = x[ds(b, 1)].rearrange("b c (r two) w -> (b c) two r w", two=2)
                above = 1 if where == "top" else 0
                half = BAND_ROWS // 2
                sp.dma_start(xband[where][0:C_IN, above:XROWS, :],
                             rows[:, 1, k * half - 1 + above:(k + 1) * half, :]).then_inc(x_loaded[where], 16)
                sp.dma_start(xband[where][C_IN:P, 0:half, :],
                             rows[:, 0, k * half:(k + 1) * half, :]).then_inc(x_loaded[where], 16)

            with sp.Fori(0, B) as b:
                load_band(b, 0, "top", -1)
                for k in range(1, BANDS):
                    load_band(b, k, buffer_of(k), k - 1 if k > 2 else k - 2)
                    if k == 3:
                        wait_apart(sp, stored[(UNITS - 1) % RING], b * (UNITS // RING * UNIT_STORES) + UNIT_STORES, idle)
                        sp.dma_start(h_txt[:], txt[ds(b, 1)].rearrange("b (t p) d -> p (b t) d", p=P)).then_inc(txt_loaded, 16)

        @block.gpsimd
        def _(pool):
            for k in ("top", "odd", "even"):
                nc.gpsimd.memset(xband[k][:], 0.0).then_inc(cleared, 1)
            for par in range(2):
                nc.gpsimd.memset(planes[par][:, 0, :, 0], 0.0).then_inc(cleared, 1)

            def planes_of(b, k):
                if k < BANDS:
                    for kx in (1, 2):
                        build_plane(pool, nc.gpsimd.tensor_copy, planes_pool, b, k, kx, wait=(kx == 1))

            def slot(b, k, more):
                if k + 1 < UNITS or more:
                    planes_of(*place(b, k + 1))

            planes_of(0, 0)
            all_units(pool, slot)

        @block.scalar
        def _(act):
            for kx in range(3):
                for ky, dst in ((0, w01[0:C_IN, kx, :]), (1, w01[C_IN:P, kx, :]), (2, w2[0:C_IN, kx, :])):
                    act.dma_start(dst, tok_w[ky, kx]).then_inc(consts_loaded, 16)
            act.dma_start(bias[:], tok_b.partition_broadcast(P)).then_inc(consts_loaded, 16)
            act.dma_start(theta_sb[:], theta.partition_broadcast(P)).then_inc(consts_loaded, 16)
            act.dma_start(id16[:], ident16).then_inc(consts_loaded, 16)
            nc.scalar.preload_act_table(ACT.Sin)

            def take_sine(b, k):
                n, par, rows = b * UNITS + k, k % 2, rows_of(k)
                act.wait_ge(arg_ready, n + 1)
                nc.scalar.activation(sine[par][0:rows], arg[par][0:rows], ACT.Sin,
                                     bias=half_pi[0:rows, 0:1]).then_inc(sine_ready, 1)

            def expand(b, k):
                n, par, rows = b * UNITS + k, k % 2, rows_of(k)
                act.wait_ge(split_ready, n + 1)
                act.wait_ge(transposed, n + 1)
                hi = q_hi[par][0:rows].rearrange("p t (h d) -> p (t h) d", d=DK).unsqueeze(2)
                lo = q_lo[par][0:rows].rearrange("p t (h d) -> p (t h) d", d=DK).unsqueeze(2)
                both = [rows, TILES * HEADS, 2, DK]
                kf = k_form[par][0:rows].rearrange("p t (h r d) -> p (t h) r d", r=4, d=DK)
                qf = q_form[par][0:rows].rearrange("p t (h r d) -> p (t h) r d", r=4, d=DK)
                for dst, src in ((kf[:, :, 0:2, :], hi), (kf[:, :, 2:4, :], lo), (qf[:, :, 0:4:2, :], hi), (qf[:, :, 1:4:2, :], lo)):
                    nc.scalar.activation(dst, src.broadcast_to(both), ACT.Copy).then_inc(forms_ready, 1)

            def evacuate(b, k):
                n, par, rows = b * UNITS + k, k % 2, rows_of(k)
                tok = TILES * rows
                act.wait_ge(transposed, n + 3)
                act.wait_ge(stored[k % RING], (b * (UNITS // RING) + k // RING) * UNIT_STORES + UNIT_STORES)
                nc.scalar.activation(k_out[k % RING][:, :, 0:tok], k_ps[:, 0:GROUPS, 0:tok], ACT.Copy).then_inc(t_evacuated, 1)
                nc.scalar.activation(q_out[k % RING][:, :, 0:tok], q_ps[:, 0:GROUPS, 0:tok], ACT.Copy).then_inc(t_evacuated, 1)
                act.wait_ge(t_evacuated, n * 2 + 4)
                at = k * BAND_TOK
                for src, dst in ((k_out, kt_s), (q_out, qt_s)):
                    act.dma_start(dst[ds(b, 1), :, :, at:at + tok].rearrange("b p g t -> (b p) g t"),
                                  src[k % RING][:, :, 0:tok]).then_inc(stored[k % RING], 16)
                act.wait_ge(split_ready, n + 1)
                for src, dst in ((h_of(k), h_s), (q[k % RING], q_s)):
                    act.dma_start(dst[ds(b * T + at, tok), :].rearrange("(t p) d -> p t d", p=rows),
                                  src[0:rows]).then_inc(stored[k % RING], 16)

            def plane_of(b, k):
                if k < BANDS:
                    build_plane(act, nc.scalar.copy, planes_act, b, k, 0, wait=True)

            def slot(b, k, more):
                if k + 1 < UNITS or more:
                    plane_of(*place(b, k + 1))
                if k >= 2:
                    evacuate(b, k - 2)
                if k < UNITS or more:
                    take_sine(*place(b, k))
                if k >= 1 and (k - 1 < UNITS or more):
                    expand(*place(b, k - 1))

            plane_of(0, 0)
            act.wait_ge(theta_arg, 1)
            nc.scalar.activation(cos_theta[:], theta_sb[:], ACT.Sin, bias=half_pi[:, 0:1]).then_inc(theta_sin, 1)
            all_units(act, slot)
            for r in range(RING):
                act.wait_ge(stored[r], (B * UNITS // RING + 1) * UNIT_STORES)

        @block.vector
        def _(dve):
            pre = Steps(dve, dve_steps)
            nc.vector.memset(w2[C_IN:P, :, :], 0.0).then_inc(cleared, 1)
            pre(nc.vector.memset(half_pi[:], math.pi / 2))
            dve.sem_inc(planes_act, 2)
            dve.sem_inc(planes_pool, 4)
            dve.sem_inc(conv_done, 2)
            dve.sem_inc(h_evacuated, 2)
            dve.sem_inc(t_evacuated, 2)
            dve.sem_inc(transposed, 2)
            dve.sem_inc(forms_ready, 2 * FORM_STEPS)
            for r in range(RING):
                dve.sem_inc(stored[r], UNIT_STORES)
            dve.wait_ge(consts_loaded, 12 * 16)
            flat = (rounds[:, 0, :], rest[:, 0, :])
            cos_argument(nc, pre, theta_sb[:], theta_sb[:], *flat)
            pre.settle()
            dve.sem_inc(theta_arg, 1)
            dve.wait_ge(theta_sin, 1)
            pre(nc.vector.tensor_scalar(cos_theta[:], cos_theta[:], Q_SCALE, None, ALU.mult))

            def front(b, k, do):
                n, par, rows = b * UNITS + k, k % 2, rows_of(k)
                dve.wait_ge(stored[k % RING], (b * (UNITS // RING) + k // RING) * UNIT_STORES + UNIT_STORES)
                if k < BANDS:
                    dve.wait_ge(conv_done, b * BANDS + k + 3)
                    ins = nc.vector.tensor_tensor(h_of(k)[0:rows], h_ps[k % 2][0:rows, :, 0:DIM],
                                                  bias[0:rows].unsqueeze(1).broadcast_to([rows, TILES, DIM]), ALU.add)
                    ins.then_inc(h_evacuated, 1)
                    dve.wait_ge(h_evacuated, b * BANDS + k + 3)
                else:
                    dve.wait_ge(txt_loaded, b * 16 + 16)
                row_stats(nc, do, idle, h_of(k), TILES, rows, stats, mv)
                row_rstd(nc, do, TILES, rows, mv, vare, rstd, tmp, tmpi)
                for t in range(TILES):
                    do(nc.vector.tensor_scalar(normed[0:rows, t, :], h_of(k)[0:rows, t, 0:HALF], mv[0:rows, t, 0:1],
                                               rstd[0:rows, t:t + 1], ALU.subtract, ALU.mult))
                cos_argument(nc, do, arg[par][0:rows], normed[0:rows], rounds[0:rows], rest[0:rows])
                do.settle()
                dve.sem_inc(arg_ready, 1)

            def back(b, k, do):
                n, par, rows = b * UNITS + k, k % 2, rows_of(k)
                dve.wait_ge(sine_ready, n + 1)
                do(nc.vector.tensor_tensor(q[k % RING][0:rows], sine[par][0:rows],
                                           cos_theta[0:rows].unsqueeze(1).broadcast_to([rows, TILES, HALF]), ALU.mult))
                do.settle()
                dve.wait_ge(forms_ready, n * FORM_STEPS + FORM_STEPS)
                do(nc.vector.tensor_copy(q_hi[par][0:rows], q[k % RING][0:rows]))
                do.settle()
                do(nc.vector.tensor_tensor(q_lo[par][0:rows], q[k % RING][0:rows], q_hi[par][0:rows], ALU.subtract))
                do.settle()
                dve.sem_inc(split_ready, 1)

            UNIT_STEPS = 3 * TILES + 1 + 11 + 5 + 3
            BACK_STEPS = 3
            FRONT_STEPS = UNIT_STEPS - BACK_STEPS
            before_2 = pre.n + 2 * FRONT_STEPS + BACK_STEPS

            def slot(b, k, more):
                if k < 2:
                    do = Steps(dve, dve_steps, pre.n + k * FRONT_STEPS)
                else:
                    do = Steps(dve, dve_steps, b * (UNITS * UNIT_STEPS) + before_2 + (k - 2) * UNIT_STEPS)
                if k < UNITS or more:
                    front(*place(b, k), do)
                if k == UNITS and not more:
                    do = Steps(dve, dve_steps, (B * UNITS - 1) * UNIT_STEPS + pre.n + FRONT_STEPS)
                if k >= 1 and (k - 1 < UNITS or more):
                    back(*place(b, k - 1), do)

            all_units(dve, slot)

        @block.tensor
        def _(pe):
            pe.wait_ge(consts_loaded, 12 * 16)
            pe.wait_ge(cleared, 6)

            def convolve(b, k):
                pe.wait_ge(planes_act, b * BANDS + k + 3)
                pe.wait_ge(planes_pool, (b * BANDS + k + 3) * 2)
                pe.wait_ge(h_evacuated, b * BANDS + max(k + 1, 2))
                for t in range(TILES):
                    for m in range(6):
                        oy, kx, w = m // 3, m % 3, (w01, w2)[m // 3]
                        at = (2 * t + oy) * SIDE
                        plane = planes[k % 2][:, kx].rearrange("p r c -> p (r c)")
                        last = nc.tensor.matmul(h_ps[k % 2][0:TILE_IMG, t, 0:DIM], plane[:, at:at + TILE_IMG], w[:, kx, :],
                                                start=(m == 0), stop=(m == 5))
                last.then_inc(conv_done, 1)

            def transpose(b, k):
                n, par, rows = b * UNITS + k, k % 2, rows_of(k)
                pe.wait_ge(forms_ready, (n + 3) * FORM_STEPS)
                pe.wait_ge(t_evacuated, n * 2 + 2)
                for form, out in ((k_form, k_ps), (q_form, q_ps)):
                    for t in range(TILES):
                        for g in range(GROUPS):
                            last = nc.tensor.transpose(out[:, g, t * rows:(t + 1) * rows],
                                                       form[par][0:rows, t, g * P:(g + 1) * P], id16[0:rows, 0:rows])
                last.then_inc(transposed, 1)

            def slot(b, k, more):
                if k < UNITS or more:
                    at = place(b, k)
                    if at[1] < BANDS:
                        convolve(*at)
                if k >= 2:
                    transpose(b, k - 2)

            all_units(pe, slot)


class ExpertWeights:

    def __init__(self, nc, ctx):
        def sb(name, shape, dt=F32):
            return ctx.enter_context(nc.sbuf_tensor(name, shape, dt))

        self.comb = sb("comb", [P, DIM])
        self.den = sb("den_select_sb", [P, P])
        self.id16 = sb("ident16_e", [P, P], F16)
        self.w_hi = sb("w_hi", [P, FORMS, STACK], F16)
        self.w_lo = sb("w_lo", [P, FORMS, STACK], F16)
        self.unscale = sb("unscale", [P, 2])
        self.b1 = sb("b1_sb", [HALF, 1])
        self.w2 = sb("w2_sb", [HALF + 1, EXPERTS])
        self.down_bias = sb("down_bias", [P, EXPERTS * CHUNK_D])
        self.up = sb("up", [P, EXPERTS * CHUNK_D, DIM])
        self.gamma = sb("gamma_sb", [P, DIM])
        self.beta = sb("beta_sb", [P, DIM])


def attention_phase(nc, q_s, kt_s, qt_s, at_s, weights, max_s, w_combine, den_select, ident16, w1, b1, w2, b2, down_w,
                    down_b, up_w, gamma, beta):
    UNITS_T = GROUPS * LANES
    HEAD_PAIRS = UNITS_T // PAIR
    SCORE_BUFS = 3
    E_SCALE = 1.0 / (Q_SCALE * Q_SCALE * math.sqrt(DK))
    K_BUF, Q_BUF, V_BUF = GROUPS * T, UNITS_T * CH, KT * HALF
    L_BUF = GROUPS * PAIR * P
    CHUNK_PAIRS = (KT - 1) * HEAD_PAIRS + GROUPS
    CHUNK_V = KT + 1
    with ExitStack() as ctx:
        def sb(name, shape, dt=F32):
            return ctx.enter_context(nc.sbuf_tensor(name, shape, dt))

        def ps(name, shape, dt=F32):
            return ctx.enter_context(nc.psum_tensor(name, shape, dt))

        def sem(name):
            return ctx.enter_context(nc.semaphore(name))

        keys = sb("keys", [P, 2 * K_BUF], F16)
        queries = sb("queries", [P, 2 * Q_BUF], F16)
        last_keys = sb("last_keys", [P, 2 * L_BUF], F16)
        all_lanes = sb("all_lanes", [P, 2 * GROUPS * CH], F16)
        values = sb("values", [P, 2 * V_BUF])
        v_tile = [sb(f"v_tile{i}", [P, GROUPS * VROW]) for i in range(3)]
        probs = sb("probs", [P, UNITS_T, CH])
        sums = sb("sums", [P, 2, CH])
        out_sb = sb("out_sb", [P, 2 * CH])
        rden = sb("rden", [P, CH])
        zeros = sb("zeros", [P, CH], F16)
        scores = [ps(f"scores{i}", [P, PAIR, 512]) for i in range(SCORE_BUFS)]
        out_ps = ps("out_ps", [P, 2, 512])

        cleared = sem("att_cleared")
        last_cleared = sem("last_cleared")
        queries_cleared = [sem(f"queries_cleared{i}") for i in range(2)]
        keys_loaded = sem("keys_loaded")
        values_loaded = sem("values_loaded")
        queries_loaded = sem("queries_loaded")
        scores_ready = sem("scores_ready")
        probs_ready = sem("probs_ready")
        pv_done = sem("pv_done")
        v_ready = sem("v_ready")
        out_evacuated = sem("out_evacuated")
        den_spread = sem("den_spread")
        out_ready = sem("out_ready")
        out_stored = sem("out_stored")
        idle = sem("idle_a")
        AHEAD = 4
        CLEARS = 4 + 4 * GROUPS + 1
        K_DMAS = (1 + LANES) * 16
        Q_DMAS = (LANES + 1) * 16
        V_DMAS = 3 * 16

        stage = sb("w_stage", [P, FORMS, STACK])
        largest, smallest = sb("w_largest", [P, 2, FORMS]), sb("w_smallest", [P, 2, FORMS])
        top, low = sb("w_top", [P, 2]), sb("w_low", [P, 2])
        all_tops = sb("w_all_tops", [P, 2 * P])
        exponent, scale_bits = sb("w_exponent", [P, 2], I32), sb("w_scale_bits", [P, 2], I32)
        comb_cleared = sem("comb_cleared")
        consts_loaded = sem("consts_loaded_e")
        stage_loaded = sem("stage_loaded")
        top_ready = sem("top_ready")
        top_stored = sem("top_stored")
        tops_loaded = sem("tops_loaded")
        split_steps = sem("split_steps")
        divide_steps = sem("divide_steps")
        N_CONSTS = LANES * GROUPS + 9

        block = ctx.enter_context(nc.Block())

        def chunk_done(c):
            return (c + 1) * (KT * GROUPS) + AHEAD

        @block.sync
        def _(sp):
            def start_keys(b):
                par = b % 2
                kdst = keys[:, par * K_BUF:(par + 1) * K_BUF].rearrange("p (g t) -> p g t", g=GROUPS)
                sp.dma_start(kdst[:, :, 0:T], kt_s[b]).then_inc(keys_loaded, 16)
                for j in range(LANES):
                    lane, column = slice(32 * j, 32 * j + 32), (j % 2) * LAST_KEYS
                    ldst = last_keys[lane, par * L_BUF:(par + 1) * L_BUF].rearrange("p (g m k) -> p g m k", g=GROUPS, m=PAIR)
                    sp.dma_start(ldst[:, :, j // 2, column:column + LAST_KEYS],
                                 kt_s[b][lane, :, T - LAST_KEYS:T]).then_inc(keys_loaded, 16)

            def start_values(b):
                par = b % 2
                vdst = values[:, par * V_BUF:(par + 1) * V_BUF].rearrange("p (t d) -> p t d", d=HALF)
                full = (KT - 1) * P
                sp.dma_start(vdst[:, 0:KT - 1, :],
                             q_s[b * T:b * T + full, :].rearrange("(t p) d -> p t d", p=P)).then_inc(values_loaded, 16)
                for half in (slice(0, LAST_KEYS), slice(LAST_KEYS, P)):
                    sp.dma_start(vdst[half, KT - 1, :], q_s[b * T + full:(b + 1) * T, :]).then_inc(values_loaded, 16)

            def batch_loaded(b):
                wait_apart(sp, keys_loaded, (b + 1) * K_DMAS, idle)
                wait_apart(sp, values_loaded, (b + 1) * V_DMAS, idle)

            def start_queries(c):
                buf = (c % 2) * Q_BUF
                for j in range(LANES):
                    lane = slice(32 * j, 32 * j + 32)
                    dst = queries[lane, ds(buf, Q_BUF)].rearrange("p (g j t) -> p g j t", g=GROUPS, j=LANES)[:, :, j, :]
                    src = qt_s[ds(c // CHUNKS, 1), lane].rearrange("b p g t -> (b p) g t")[:, :, ds(c % CHUNKS * CH, CH)]
                    sp.dma_start(dst, src).then_inc(queries_loaded, 16)
                dst = all_lanes[:, ds((c % 2) * (GROUPS * CH), GROUPS * CH)].rearrange("p (g t) -> p g t", g=GROUPS)
                src = qt_s[ds(c // CHUNKS, 1)].rearrange("b p g t -> (b p) g t")[:, :, ds(c % CHUNKS * CH, CH)]
                sp.dma_start(dst, src).then_inc(queries_loaded, 16)

            def load_batch(b):
                start_keys(b)
                start_values(b)
                batch_loaded(b)

            def load_queries(c):
                start_queries(c)
                wait_apart(sp, queries_loaded, c * Q_DMAS + Q_DMAS, idle)

            def store_out(c):
                wait_apart(sp, out_ready, c + 3, idle)
                sp.dma_start(at_s[:, ds(c * CH, CH)], out_sb[:, ds(c % 2 * CH, CH)]).then_inc(out_stored, 16)
                wait_apart(sp, out_stored, c * 16 + 64, idle)

            def load_weights():
                for k, row, feature, n in STACK_ROWS:
                    rows, features = slice(row, row + n), slice(feature, feature + n)
                    sp.dma_start(stage[rows, k, 0:GATE_AT].rearrange("p (e d) -> p e d", e=EXPERTS),
                                 down_w[:, features, :].rearrange("e p d -> p e d")).then_inc(stage_loaded, 16)
                    sp.dma_start(stage[rows, k, GATE_AT:STACK], w1[features, :]).then_inc(stage_loaded, 16)

                def const(dst, src):
                    sp.dma_start(dst, src).then_inc(consts_loaded, 16)

                sp.wait_ge(comb_cleared, 1)
                for j in range(LANES):
                    for g in range(GROUPS):
                        at, row = 32 * j + DK * g, (LANES * g + j) * DK
                        const(weights.comb[at:at + DK, :], w_combine[row:row + DK, :])
                const(weights.den[:], den_select)
                const(weights.id16[:], ident16)
                const(weights.b1[:], b1.rearrange("(p a) -> p a", a=1))
                const(weights.w2[0:HALF, :], w2)
                const(weights.w2[HALF:HALF + 1, :], b2.rearrange("(a e) -> a e", a=1))
                const(weights.down_bias[:], down_b)
                const(weights.up[:], up_w.rearrange("e (c p) h -> p (e c) h", c=CHUNK_D))
                const(weights.gamma[:], gamma.partition_broadcast(P))
                const(weights.beta[:], beta.partition_broadcast(P))
                sp.wait_ge(top_ready, 1)
                sp.dma_start(max_s, top[:]).then_inc(top_stored, 16)
                sp.wait_ge(top_stored, 16)
                sp.dma_start(all_tops[:], max_s.rearrange("p r -> (p r)").partition_broadcast(P)).then_inc(tops_loaded, 16)

            sp.wait_ge(last_cleared, 1)
            start_keys(0)
            sp.wait_ge(queries_cleared[0], 1)
            start_queries(0)
            start_values(0)
            wait_apart(sp, queries_loaded, Q_DMAS, idle)
            sp.wait_ge(queries_cleared[1], 1)
            load_queries(1)
            batch_loaded(0)
            load_batch(1)
            load_weights()
            for b in range(B):
                if 1 <= b < B - 1:
                    load_batch(b + 1)
                with sp.Fori(b * CHUNKS + 2, min((b + 1) * CHUNKS + 2, NCHUNK)) as c:
                    wait_apart(sp, pv_done, chunk_done(c - 2), idle)
                    load_queries(c)
                    store_out(c - 2)
            sp.sem_inc(queries_loaded, Q_DMAS)
            sp.sem_inc(keys_loaded, K_DMAS)
            store_out(NCHUNK - 2)
            store_out(NCHUNK - 1)
            sp.wait_ge(consts_loaded, N_CONSTS * 16)

        @block.vector
        def _(dve):
            def split_weights():
                do = Steps(dve, split_steps)
                parts = (slice(0, GATE_AT), slice(GATE_AT, STACK))
                dve.wait_ge(stage_loaded, 2 * len(STACK_ROWS) * 16)
                for i, part in enumerate(parts):
                    do(nc.vector.tensor_reduce(largest[:, i, :], stage[:, :, part], AX_X, ALU.max))
                    do(nc.vector.tensor_reduce(smallest[:, i, :], stage[:, :, part], AX_X, ALU.min))
                do.settle()
                do(nc.vector.tensor_reduce(top[:], largest[:], AX_X, ALU.max))
                do(nc.vector.tensor_reduce(low[:], smallest[:], AX_X, ALU.min))
                do.settle()
                do(nc.vector.scalar_tensor_tensor(top[:], low[:], -1.0, top[:], ALU.mult, ALU.max))
                do.settle()
                dve.sem_inc(top_ready, 1)
                dve.wait_ge(tops_loaded, 16)
                do(nc.vector.tensor_reduce(low[:], all_tops[:].rearrange("p (q r) -> p r q", r=2), AX_X, ALU.max))
                do.settle()
                do(nc.vector.tensor_scalar(exponent[:], low[:].bitcast(I32), 23, None, ALU.logical_shift_right))
                do.settle()
                do(nc.vector.tensor_scalar(exponent[:], exponent[:], -1.0, 254.0 + W_EXPONENT, ALU.mult, ALU.add))
                do.settle()
                do(nc.vector.tensor_scalar(scale_bits[:], exponent[:], float(MAX_SCALE_BITS), float(1 << 23), ALU.min, ALU.mult))
                do.settle()
                do(nc.vector.tensor_scalar(weights.unscale[:].bitcast(I32), scale_bits[:], -1.0,
                                           float((254 - Y_SCALE_LOG2) << 23), ALU.mult, ALU.add))
                scale = scale_bits[:].bitcast(F32)
                for i, part in enumerate(parts):
                    do(nc.vector.tensor_scalar(weights.w_hi[:, :, part], stage[:, :, part], scale[:, i:i + 1], None, ALU.mult))
                do.settle()
                for i, part in enumerate(parts):
                    do(nc.vector.scalar_tensor_tensor(weights.w_lo[:, :, part], stage[:, :, part], scale[:, i:i + 1],
                                                      weights.w_hi[:, :, part], ALU.mult, ALU.subtract))
                do.settle()

            nc.vector.memset(last_keys[:].bitcast(F32), 0.0).then_inc(last_cleared, 1)
            nc.vector.memset(queries[:, 0:Q_BUF].bitcast(F32), 0.0).then_inc(queries_cleared[0], 1)
            for buf in (zeros, *v_tile):
                nc.vector.memset(buf[:], 0.0).then_inc(cleared, 1)
            dve.wait_ge(cleared, 4)
            for i, rows, lanes in ((0, slice(0, P), slice(0, LANES)), (1, slice(0, P), slice(0, LANES)),
                                   (2, slice(0, LAST_KEYS), slice(0, LANES, 2)), (2, slice(LAST_KEYS, P), slice(1, LANES, 2))):
                for g in range(GROUPS):
                    strips = v_tile[i][rows, g * P:(g + 1) * P].rearrange("p (j x) -> p j x", x=32)
                    nc.vector.memset(strips[:, lanes, 3 * DK + g], Q_SCALE).then_inc(cleared, 1)
            nc.vector.memset(sums[:], 1.0).then_inc(cleared, 1)
            dve.sem_inc(out_evacuated, 2)
            dve.sem_inc(out_stored, 48)
            dve.sem_inc(out_ready, 1)
            dve.sem_inc(pv_done, AHEAD)
            nc.vector.memset(weights.comb[:], 0.0).then_inc(comb_cleared, 1)
            split_weights()

            def divide(done, par):
                dve.wait_ge(den_spread, done + 1)
                dve.wait_ge(out_stored, done * 16 + 16)
                nc.vector.reciprocal(rden[:], out_ps[:, par, 0:CH]).then_inc(divide_steps, 1)
                dve.wait_ge(divide_steps, done + 1)
                nc.vector.tensor_tensor(out_sb[:, par * CH:(par + 1) * CH], sums[:, par, :], rden[:],
                                        ALU.mult).then_inc(out_ready, 1)
                dve.wait_ge(out_ready, done + 2)

            with dve.Fori(0, NCHUNK // 2) as m:
                for par in range(2):
                    divide(m * 2 + par, 1 - par)
                    dve.wait_ge(pv_done, chunk_done(m * 2 + par))
                    nc.vector.tensor_copy(sums[:, par, :], out_ps[:, par, 0:CH]).then_inc(out_evacuated, 1)
            divide(NCHUNK, 1)

        @block.gpsimd
        def _(pool):
            nc.gpsimd.memset(queries[:, Q_BUF:2 * Q_BUF].bitcast(F32), 0.0).then_inc(queries_cleared[1], 1)
            pool.wait_ge(cleared, CLEARS)

            def place_values(tile, rows, lanes, start):
                dst = v_tile[tile][rows].rearrange("p (g r) -> p g r", r=VROW)[:, :, 0:P]
                dst = dst.rearrange("p g (j x) -> p g j x", x=32)[:, :, lanes, 0:DK]
                src = values[rows, ds(start, HALF)].rearrange("p (g j d) -> p g j d", g=GROUPS, j=LANES)[:, :, lanes, :]
                nc.gpsimd.tensor_copy(dst, src).then_inc(v_ready, 1)

            def tile_free(n):
                wait_apart(pool, pv_done, n * GROUPS + (AHEAD - GROUPS), idle)

            with pool.Fori(0, NCHUNK) as c:
                buf = (c // CHUNKS % 2) * V_BUF
                wait_apart(pool, values_loaded, (c // CHUNKS) * V_DMAS + V_DMAS, idle)
                with pool.Fori(0, PAIRS) as i:
                    for x in range(2):
                        tile_free(c * KT + i * 2 + x)
                        place_values(x, slice(0, P), slice(0, LANES), buf + i * (2 * HALF) + x * HALF)
                tile_free(c * KT + KT - 1)
                place_values(2, slice(0, LAST_KEYS), slice(0, LANES, 2), buf + (KT - 1) * HALF)
                wait_apart(pool, v_ready, c * CHUNK_V + (CHUNK_V - 1), idle)
                place_values(2, slice(LAST_KEYS, P), slice(1, LANES, 2), buf + (KT - 1) * HALF)
                wait_apart(pool, v_ready, c * CHUNK_V + CHUNK_V, idle)

        @block.scalar
        def _(act):
            nc.scalar.preload_act_table(ACT.Exp)

            def exps(n, pairs, packed=False):
                for k in range(GROUPS if packed else HEAD_PAIRS):
                    act.wait_ge(scores_ready, pairs + (k + 1))
                    first = LANES * k if packed else PAIR * k
                    act.wait_ge(pv_done, n * GROUPS + (first // LANES + 1 + AHEAD - GROUPS))
                    nc.scalar.activation(probs[:, first:first + PAIR, :], scores[k % SCORE_BUFS][:, :, 0:CH],
                                         ACT.Exp, scale=E_SCALE).then_inc(probs_ready, 1)

            with act.Fori(0, NCHUNK) as c:
                with act.Fori(0, PAIRS) as i:
                    for x in range(2):
                        exps(c * KT + i * 2 + x, c * CHUNK_PAIRS + i * (2 * HEAD_PAIRS) + x * HEAD_PAIRS)
                exps(c * KT + KT - 1, c * CHUNK_PAIRS + (KT - 1) * HEAD_PAIRS, packed=True)

        @block.tensor
        def _(pe):
            def score(k, key_at, query_at):
                for m in range(PAIR):
                    u = PAIR * k + m
                    last = nc.tensor.matmul(scores[k % SCORE_BUFS][:, m, 0:CH], keys[:, ds(key_at + (u // LANES) * T, P)],
                                            queries[:, ds(query_at + u * CH, CH)], start=True, stop=True)
                last.then_inc(scores_ready, 1)

            def score_packed(g, last_key_at, lanes_at):
                for m in range(PAIR):
                    last = nc.tensor.matmul(scores[g % SCORE_BUFS][:, m, 0:CH], last_keys[:, ds(last_key_at + (g * PAIR + m) * P, P)],
                                            all_lanes[:, ds(lanes_at + g * CH, CH)], start=True, stop=True)
                last.then_inc(scores_ready, 1)

            def weigh(g, tile, par, packed=False):
                for j in range(LANES):
                    at, place = g * P + 32 * j, LANES * g + (j // 2 if packed else j)
                    last = nc.tensor.matmul(out_ps[32 * j:32 * j + 32, par, 0:CH], v_tile[tile][:, at:at + 32],
                                            probs[:, place, :], start=False, stop=(packed and g == GROUPS - 1))
                last.then_inc(pv_done, 1)

            def key_tile(pairs, values_placed, here, after, tile, par, next_packed=False):
                for g in range(GROUPS):
                    for k in (2 * g, 2 * g + 1):
                        pe.wait_ge(probs_ready, pairs + (k + 1))
                        ahead = k + SCORE_BUFS
                        if ahead < HEAD_PAIRS:
                            score(ahead, *here)
                        else:
                            (score_packed if next_packed else score)(ahead - HEAD_PAIRS, *after)
                    if g == 0:
                        pe.wait_ge(v_ready, values_placed)
                    weigh(g, tile, par)

            def last_tile(pairs, values_placed, after, par):
                for g in range(GROUPS):
                    pe.wait_ge(probs_ready, pairs + (g + 1))
                    score(g, *after)
                    if g == 0:
                        pe.wait_ge(v_ready, values_placed)
                    weigh(g, 2, par, packed=True)

            def two_tiles(c, i, k_buf, q_buf, par, packed=None):
                at, pairs, placed = k_buf + i * (2 * P), c * CHUNK_PAIRS + i * (2 * HEAD_PAIRS), c * CHUNK_V + i * 2
                key_tile(pairs, placed + 1, (at, q_buf), (at + P, q_buf), 0, par)
                key_tile(pairs + HEAD_PAIRS, placed + 2, (at + P, q_buf), packed or (at + 2 * P, q_buf),
                         1, par, next_packed=packed is not None)

            def spread_denominators(chunks, par):
                pe.wait_ge(out_evacuated, chunks + 2)
                nc.tensor.matmul(out_ps[:, par, 0:CH], weights.den[:], sums[:, par, :], start=True, stop=True).then_inc(den_spread, 1)

            pe.wait_ge(cleared, CLEARS)
            pe.wait_ge(keys_loaded, K_DMAS)
            pe.wait_ge(queries_loaded, Q_DMAS)
            for k in range(SCORE_BUFS):
                score(k, 0, 0)
            with pe.Fori(0, NCHUNK // 2) as m:
                for par in range(2):
                    c = m * 2 + par
                    k_buf, q_buf = (m // (CHUNKS // 2) % 2) * K_BUF, par * Q_BUF
                    next_k, next_q = ((c + 1) // CHUNKS % 2) * K_BUF, (1 - par) * Q_BUF
                    pe.wait_ge(out_ready, c + 1)
                    nc.tensor.matmul(out_ps[:, par, 0:CH], zeros[:, 0:P], zeros[:], start=True, stop=False)
                    with pe.Fori(0, PAIRS - 1) as i:
                        two_tiles(c, i, k_buf, q_buf, par)
                    pe.wait_ge(consts_loaded, N_CONSTS * 16)
                    spread_denominators(c, 1 - par)
                    two_tiles(c, PAIRS - 1, k_buf, q_buf, par, ((m // (CHUNKS // 2) % 2) * L_BUF, par * (GROUPS * CH)))
                    pe.wait_ge(queries_loaded, c * Q_DMAS + 2 * Q_DMAS)
                    pe.wait_ge(keys_loaded, ((c + 1) // CHUNKS) * K_DMAS + K_DMAS)
                    last_tile(c * CHUNK_PAIRS + (KT - 1) * HEAD_PAIRS, c * CHUNK_V + CHUNK_V, (next_k, next_q), par)
            spread_denominators(NCHUNK, 1)


def experts_phase(nc, h_s, at_s, weights, out):
    UP_RING = 4
    UPS = EXPERTS * ST
    with ExitStack() as ctx:
        def sb(name, shape, dt=F32):
            return ctx.enter_context(nc.sbuf_tensor(name, shape, dt))

        def ps(name, shape, dt=F32):
            return ctx.enter_context(nc.psum_tensor(name, shape, dt))

        def sem(name):
            return ctx.enter_context(nc.semaphore(name))

        h_in = [sb(f"h_in{i}", [P, ST, DIM]) for i in range(2)]
        att = [sb(f"att{i}", [P, SN]) for i in range(2)]
        h2 = [sb(f"h2_{i}", [P, ST, DIM]) for i in range(2)]
        h2_beta = [sb(f"h2_beta{i}", [P, ST, DIM]) for i in range(2)]
        y = [sb(f"y{i}", [P, ST, DIM]) for i in range(2)]
        y_parts = sb("y_parts", [P, ST, 2 * DIM], F16)
        yt = [sb(f"yt{i}", [P, FORMS, SN], F16) for i in range(2)]
        hid = sb("hid", [HALF + 1, SN])
        logit = sb("logit", [P, ST, EXPERTS])
        expo = sb("expo", [P, ST, EXPERTS])
        route = sb("route", [P, ST, 2 * EXPERTS])
        top = sb("top", [P, ST, EXPERTS])
        pick = sb("pick", [P, ST, EXPERTS])
        left = sb("left", [P, ST, 2 * EXPERTS])
        gates = [sb(f"gates{i}", [P, ST, EXPERTS]) for i in range(2)]
        s1, s2 = sb("s1", [P, ST]), sb("s2", [P, ST])
        zt = [sb(f"zt{i}", [P, CHUNK_D, SN]) for i in range(2)]
        moe = [sb(f"moe{i}", [P, ST, DIM]) for i in range(2)]
        fin = [sb(f"fin{i}", [P, ST, DIM]) for i in range(2)]
        stats = sb("stats_e", [P, ST, 6])
        mv = sb("mv_e", [P, ST, 2])
        vare, rstd, tmp = (sb(n, [P, ST]) for n in ("vare_e", "rstd_e", "tmp_e"))
        tmpi = sb("tmpi_e", [P, ST], I32)

        z_ps = [ps(f"z_ps{i}", [P, CHUNK_D, 512]) for i in range(2)]
        up_ps = ps("up_ps", [P, UP_RING, 256])
        pre_ps = ps("pre_ps", [P, 2, 512])
        pre_half = pre_ps[:].rearrange("p b x -> p (b x)").bitcast(F16).rearrange("p (k x) -> p k x", x=512)
        pre_tiles = pre_ps[:].rearrange("p b (t x) -> p (b t) x", x=256)

        cleared = sem("cleared_e")
        loaded = [sem(f"loaded{i}") for i in range(2)]
        pre_mm = sem("pre_mm")
        pre_act = sem("pre_act")
        pre_dve = sem("pre_dve")
        down_done = sem("down_done")
        z_ready = sem("z_ready")
        up_done = sem("up_done")
        added = sem("added")
        fin_ready = sem("fin_ready")
        beta_added = sem("beta_added")
        fin_steps = sem("fin_steps")
        stored = [sem(f"out_stored{i}") for i in range(2)]
        dve_steps = sem("dve_steps_e")
        idle = sem("idle_e")

        block = ctx.enter_context(nc.Block())

        def all_supertiles(eng, body):
            body(0, 0, 0, False, True)
            with eng.Fori(0, NSUPER // 2 - 1) as i:
                body(i * 2 + 1, 1, i, True, True)
                body(i * 2 + 2, 0, i + 1, True, True)
            body(NSUPER - 1, 1, NSUPER // 2 - 1, True, False)

        @block.sync
        def _(sp):
            def load(s, par):
                sp.dma_start(att[par][:], at_s[:, ds(s * SN, SN)]).then_inc(loaded[par], 16)
                sp.dma_start(h_in[par][:], h_s[ds(s * SN, SN), :].rearrange("(t p) d -> p t d", p=P)).then_inc(loaded[par], 16)

            load(0, 0)
            load(1, 1)

            def load_next(s, par):
                wait_apart(sp, pre_dve, s * 2 + 2, idle)
                load(s + 2, par)

            def store(s, par):
                wait_apart(sp, fin_steps, s * 2 + 2, idle)
                sp.dma_start(out[ds(s * SN, SN), :].rearrange("(t p) d -> p t d", p=P), fin[par][:]).then_inc(stored[par], 16)

            with sp.Fori(0, NSUPER // 2 - 1) as i:
                for par in range(2):
                    load_next(i * 2 + par, par)
                    store(i * 2 + par, par)
            for par in range(2):
                store(NSUPER - 2 + par, par)
            for par in range(2):
                sp.wait_ge(stored[par], (NSUPER // 2) * 16 + 16)

        @block.gpsimd
        def _(pool):
            wide = [P, ST, DIM]

            def add_beta(s, par):
                wait_apart(pool, pre_dve, s * 2 + 2, idle)
                nc.gpsimd.tensor_tensor(h2_beta[par][:], h2[par][:], weights.beta[:].unsqueeze(1).broadcast_to(wide),
                                        ALU.add).then_inc(beta_added, 1)

            def finish(s, par):
                wait_apart(pool, fin_ready, s + 1, idle)
                nc.gpsimd.tensor_tensor(fin[par][:], fin[par][:], weights.gamma[:].unsqueeze(1).broadcast_to(wide),
                                        ALU.mult).then_inc(fin_steps, 1)
                wait_apart(pool, fin_steps, s * 2 + 1, idle)
                wait_apart(pool, beta_added, s + 1, idle)
                nc.gpsimd.tensor_tensor(fin[par][:], fin[par][:], h2_beta[par][:], ALU.add).then_inc(fin_steps, 1)

            def body(s, par, m, has_prev, has_next):
                if has_prev:
                    finish(s - 1, 1 - par)
                if has_next:
                    if has_prev:
                        wait_apart(pool, fin_steps, s * 2, idle)
                    add_beta(s + 1, 1 - par)

            add_beta(0, 0)
            all_supertiles(pool, body)
            finish(NSUPER - 1, 1)

        @block.scalar
        def _(act):
            nc.scalar.preload_act_table(ACT.Gelu)

            def copy_yt(s, par):
                act.wait_ge(pre_mm, s * 4 + 2)
                nc.scalar.activation(yt[par][:], pre_half[:, 0:FORMS, 0:SN], ACT.Copy).then_inc(pre_act, 1)

            def gate_hidden(s):
                act.wait_ge(pre_mm, s * 4 + 3)
                nc.scalar.activation(hid[0:HALF, :], pre_ps[0:HALF, 0, 0:SN], ACT.Gelu,
                                     bias=weights.b1[:, 0:1], scale=weights.unscale[0:HALF, 1:2]).then_inc(pre_act, 1)

            def gate_exp(s):
                act.wait_ge(pre_dve, s * 2 + 3)
                nc.scalar.activation(expo[:], logit[:], ACT.Exp).then_inc(pre_act, 1)

            def body(s, par, m, has_prev, has_next):
                for e in range(EXPERTS):
                    act.wait_ge(down_done, s * EXPERTS + (e + 1))
                    act.wait_ge(up_done, s * UPS + (e + 1) * ST)
                    for c in range(CHUNK_D):
                        col = e * CHUNK_D + c
                        last = nc.scalar.activation(zt[e % 2][:, c, :], z_ps[e % 2][:, c, 0:SN], ACT.Gelu,
                                                    bias=weights.down_bias[:, col:col + 1], scale=weights.unscale[:, 0:1])
                    last.then_inc(z_ready, 1)
                    if has_next and e == 4:
                        copy_yt(s + 1, 1 - par)
                    if has_next and e == 5:
                        gate_hidden(s + 1)
                if has_next:
                    gate_exp(s + 1)

            copy_yt(0, 0)
            gate_hidden(0)
            gate_exp(0)
            all_supertiles(act, body)

        @block.vector
        def _(dve):
            nc.vector.memset(hid[HALF:HALF + 1, :], 1.0).then_inc(cleared, 1)
            do = Steps(dve, dve_steps)
            do(nc.vector.memset(route[:], -1.0))
            do(nc.vector.memset(pick[:], -1.0))
            dve.sem_inc(pre_dve, 1)
            dve.sem_inc(z_ready, 2)
            dve.sem_inc(up_done, 2 * ST)
            dve.sem_inc(added, UP_RING)
            dve.sem_inc(stored[0], 16)
            dve.sem_inc(stored[1], 16)

            def residual(s, par):
                dve.wait_ge(pre_mm, s * 4 + 1)
                do(nc.vector.tensor_tensor(h2[par][:], pre_tiles[:, 0:ST, 0:DIM], h_in[par][:], ALU.add))

            def norm(par):
                row_stats(nc, do, idle, h2[par], ST, P, stats, mv)
                row_rstd(nc, do, ST, P, mv, vare, rstd, tmp, tmpi)
                for t in range(ST):
                    last = nc.vector.tensor_scalar(y[par][:, t, :], h2[par][:, t, :], mv[:, t, 0:1], rstd[:, t:t + 1],
                                                   ALU.subtract, ALU.mult)
                    do(last)

            def split_y(par):
                do.settle()
                do(nc.vector.tensor_scalar(y_parts[:, :, 0:DIM], y[par][:], float(1 << Y_SCALE_LOG2), None, ALU.mult))
                do.settle()
                nc.vector.scalar_tensor_tensor(y_parts[:, :, DIM:2 * DIM], y[par][:], float(1 << Y_SCALE_LOG2),
                                               y_parts[:, :, 0:DIM], ALU.mult, ALU.subtract).then_inc(pre_dve, 1)

            def norm_out_stats(s, par):
                dve.wait_ge(added, (s + 1) * UPS + UP_RING)
                row_stats(nc, do, idle, moe[par], ST, P, stats, mv)
                row_rstd(nc, do, ST, P, mv, vare, rstd, tmp, tmpi)

            def norm_out(par, m):
                dve.wait_ge(stored[par], m * 16 + 16)
                for t in range(ST):
                    do(nc.vector.tensor_scalar(fin[par][:, t, :], moe[par][:, t, :], mv[:, t, 0:1], rstd[:, t:t + 1],
                                               ALU.subtract, ALU.mult))
                do.settle()
                dve.sem_inc(fin_ready, 1)

            def gate_logits(s):
                dve.wait_ge(pre_mm, s * 4 + 4)
                lg = pre_ps[:, 1, 0:ST * EXPERTS].rearrange("p (t e) -> p t e", e=EXPERTS)
                do(nc.vector.tensor_reduce(s1[:], lg, AX_X, ALU.max))
                do.settle()
                nc.vector.tensor_tensor(logit[:], lg, s1[:].unsqueeze(2).broadcast_to([P, ST, EXPERTS]),
                                        ALU.subtract).then_inc(pre_dve, 1)

            def gate_top2(s, par):
                wide = [P, ST, EXPERTS]
                dve.wait_ge(pre_act, s * 3 + 3)
                do(nc.vector.tensor_reduce(s1[:], expo[:], AX_X, ALU.add))
                do.settle()
                do(nc.vector.reciprocal(s2[:], s1[:]))
                do.settle()
                do(nc.vector.tensor_tensor(route[:, :, 0:EXPERTS], expo[:], s2[:].unsqueeze(2).broadcast_to(wide), ALU.mult))
                do.settle(idle)
                for t in range(ST):
                    do(nc.vector.max(top[:, t, :], route[:, t, 0:EXPERTS]))
                do.settle()
                do(nc.vector.tensor_copy(pick[:, :, 0:2], top[:, :, 0:2]))
                do.settle(idle)
                for t in range(ST):
                    do(nc.vector.match_replace(left[:, t, :], pick[:, t, :], route[:, t, :], 0.0))
                do.settle()
                do(nc.vector.tensor_tensor(top[:], route[:, :, 0:EXPERTS], left[:, :, 0:EXPERTS], ALU.subtract))
                do.settle()
                do(nc.vector.tensor_reduce(s1[:], top[:], AX_X, ALU.add))
                do.settle()
                do(nc.vector.tensor_scalar(s1[:], s1[:], GATE_EPS, None, ALU.add))
                do.settle()
                do(nc.vector.reciprocal(s2[:], s1[:]))
                do.settle()
                do(nc.vector.tensor_tensor(gates[par][:], top[:], s2[:].unsqueeze(2).broadcast_to(wide), ALU.mult))
                do.settle()

            LN_STEPS = 2 * ST + 1 + 11
            GATE_STEPS = 3 + ST + 1 + ST + 5
            OUT_STEPS = LN_STEPS + ST
            PRE_STEPS = 1 + LN_STEPS + ST + 1 + 1 + GATE_STEPS
            SUPER_STEPS = OUT_STEPS + PRE_STEPS
            start_steps = 2 + PRE_STEPS
            RESIDUAL_AT, NORM_AT, SPLIT_AT, STATS_AT, OUT_AT, LOGITS_AT = 1, 2, 3, 6, 8, 9

            def body(s, par, m, has_prev, has_next):
                nonlocal do
                do = Steps(dve, dve_steps, start_steps + s * SUPER_STEPS - (OUT_STEPS if has_prev else 0))
                for bank in range(UPS // 2):
                    do.settle()
                    dve.wait_ge(up_done, s * UPS + (2 * bank + 2 + 2 * ST))
                    for r in (2 * bank, 2 * bank + 1):
                        e, t = r // ST, r % ST
                        if e:
                            dve.wait_ge(added, s * UPS + (r + 1 - ST + UP_RING))
                        so_far = moe[par][:, t, :] if e else y[par][:, t, :]
                        nc.vector.scalar_tensor_tensor(moe[par][:, t, :], up_ps[:, r % UP_RING, 0:DIM],
                                                       gates[par][:, t, e:e + 1], so_far, ALU.mult, ALU.add).then_inc(added, 1)
                    if has_next and bank == RESIDUAL_AT:
                        if has_prev:
                            dve.wait_ge(beta_added, s)
                        residual(s + 1, 1 - par)
                    if has_next and bank == NORM_AT:
                        norm(1 - par)
                    if has_next and bank == SPLIT_AT:
                        split_y(1 - par)
                    if has_prev and bank == STATS_AT:
                        norm_out_stats(s - 1, 1 - par)
                    if has_prev and bank == OUT_AT:
                        norm_out(1 - par, m + par - 1)
                    if has_next and bank == LOGITS_AT:
                        gate_logits(s + 1)
                if has_next:
                    gate_top2(s + 1, 1 - par)
                    assert do.n == SUPER_STEPS - (0 if has_prev else OUT_STEPS)

            dve.wait_ge(loaded[0], 32)
            residual(0, 0)
            norm(0)
            split_y(0)
            gate_logits(0)
            gate_top2(0, 0)
            assert do.n == start_steps
            all_supertiles(dve, body)
            norm_out_stats(NSUPER - 1, 1)
            norm_out(1, NSUPER // 2 - 1)

        @block.tensor
        def _(pe):
            pe.wait_ge(cleared, 1)

            def project(s, par):
                pe.wait_ge(pre_dve, s * 2 + 1)
                for t in range(ST):
                    last = nc.tensor.matmul(pre_tiles[:, t, 0:DIM], att[par][:, t * P:(t + 1) * P], weights.comb[:],
                                            start=True, stop=True)
                last.then_inc(pre_mm, 1)

            def times_y(out, par, columns):
                parts = [(w, k) for w in (weights.w_hi, weights.w_lo) for k in range(FORMS)]
                for w, k in parts:
                    last = nc.tensor.matmul(out, w[:, k, columns], yt[par][:, k, :], start=((w, k) == parts[0]),
                                            stop=((w, k) == parts[-1]))
                return last

            def transpose_y(s):
                pe.wait_ge(pre_dve, s * 2 + 2)
                for k in range(FORMS):
                    for t in range(ST):
                        last = nc.tensor.transpose(pre_half[:, k, t * P:(t + 1) * P], y_parts[:, t, k * P:(k + 1) * P],
                                                   weights.id16[:])
                last.then_inc(pre_mm, 1)

            def gate_hidden(s, par):
                pe.wait_ge(pre_act, s * 3 + 1)
                times_y(pre_ps[0:HALF, 0, 0:SN], par, slice(GATE_AT, STACK)).then_inc(pre_mm, 1)

            def gate_logits(s):
                pe.wait_ge(pre_act, s * 3 + 2)
                for t in range(ST):
                    last = nc.tensor.matmul(pre_ps[:, 1, t * EXPERTS:(t + 1) * EXPERTS], hid[:, t * P:(t + 1) * P], weights.w2[:],
                                            start=True, stop=True)
                last.then_inc(pre_mm, 1)

            def go_down(s, par, e):
                pe.wait_ge(z_ready, s * EXPERTS + (e + 1))
                for c in range(CHUNK_D):
                    at = (e * CHUNK_D + c) * P
                    last = times_y(z_ps[e % 2][:, c, 0:SN], par, slice(at, at + P))
                last.then_inc(down_done, 1)

            def go_up(s, e):
                pe.wait_ge(z_ready, s * EXPERTS + (e + 3))
                for t in range(ST):
                    r = e * ST + t
                    if r % 2 == 0:
                        pe.wait_ge(added, s * UPS + (r + 2))
                    for c in range(CHUNK_D):
                        last = nc.tensor.matmul(up_ps[:, r % UP_RING, 0:DIM], zt[e % 2][:, c, t * P:(t + 1) * P],
                                                weights.up[:, e * CHUNK_D + c, :], start=(c == 0), stop=(c == CHUNK_D - 1))
                    last.then_inc(up_done, 1)

            def body(s, par, m, has_prev, has_next):
                go_down(s, par, 0)
                for e in range(EXPERTS):
                    if e + 1 < EXPERTS:
                        go_down(s, par, e + 1)
                    if has_next and e == 0:
                        pe.wait_ge(loaded[1 - par], (m + par + 1) * 32)
                        project(s + 1, 1 - par)
                    if has_next and e == 4:
                        transpose_y(s + 1)
                    if has_next and e == 5:
                        gate_hidden(s + 1, 1 - par)
                    if has_next and e == 6:
                        gate_logits(s + 1)
                    go_up(s, e)

            pe.wait_ge(loaded[0], 32)
            project(0, 0)
            transpose_y(0)
            gate_hidden(0, 0)
            gate_logits(0)
            all_supertiles(pe, body)


def fusion_kernel(nc, x, txt, tok_w, tok_b, theta, w_combine, w1, b1, w2, b2, down_w, down_b, up_w, gamma, beta,
                  ident16, den_select, out):
    h_s = nc.dram_tensor("h_scratch", (NTOK, DIM), F32).ap()
    q_s = nc.dram_tensor("q_scratch", (NTOK, HALF), F32).ap()
    kt_s = nc.dram_tensor("keys_scratch", (B, P, GROUPS, T), F16).ap()
    qt_s = nc.dram_tensor("queries_scratch", (B, P, GROUPS, T), F16).ap()
    at_s = nc.dram_tensor("attention_scratch", (P, NTOK), F32).ap()
    tokens_phase(nc, x, txt, tok_w, tok_b, theta, ident16, h_s, q_s, kt_s, qt_s)
    max_s = nc.dram_tensor("largest_weights_scratch", (P, 2), F32).ap()
    with ExitStack() as ctx:
        weights = ExpertWeights(nc, ctx)
        attention_phase(nc, q_s, kt_s, qt_s, at_s, weights, max_s, w_combine, den_select, ident16, w1, b1, w2, b2, down_w,
                        down_b, up_w, gamma, beta)
        experts_phase(nc, h_s, at_s, weights, out.rearrange("b t d -> (b t) d"))


def _denominator_rows():
    select = np.zeros((P, P), np.float32)
    for m in range(P):
        j, r = divmod(m, 32)
        g = r // DK if r < GROUPS * DK else min(r - GROUPS * DK, 0)
        select[32 * j + GROUPS * DK + g, m] = 1.0
    return select


def kernel(**inputs):
    import concourse.bacc as bacc
    from concourse.bass_utils import run_bass_kernel_spmd

    given = {k: np.asarray(v) for k, v in inputs.items()}
    arrays = {
        "x": given["x"],
        "txt": given["txt"],
        "tok_w": np.ascontiguousarray(given["L0_tok_W"].reshape(DIM, C_IN, 3, 3).transpose(2, 3, 1, 0)),
        "tok_b": given["L0_tok_b"],
        "theta": given["L0_attn_theta"],
        "w_combine": np.ascontiguousarray(given["L0_attn_W_combine"].T),
        "w1": given["L0_ffn_w1"],
        "b1": given["L0_ffn_b1"],
        "w2": given["L0_ffn_w2"],
        "b2": given["L0_ffn_b2"],
        "down_w": given["L0_ffn_down_w"],
        "down_b": np.ascontiguousarray(given["L0_ffn_down_b"].reshape(-1, P).T),
        "up_w": given["L0_ffn_up_w"],
        "gamma": given["L0_ffn_gamma"],
        "beta": given["L0_ffn_beta"],
        "ident16": np.eye(P, dtype=np.float16),
        "den_select": _denominator_rows(),
    }
    nc = bacc.Bacc("TRN2", target_bir_lowering=False, num_devices=1)
    in_maps, args = {}, []
    for name, a in arrays.items():
        in_maps[f"in_{name}"] = a
        args.append(nc.dram_tensor(f"in_{name}", a.shape, mybir.dt.from_np(a.dtype), kind="ExternalInput").ap())
    args.append(nc.dram_tensor("out_0", (B, T, DIM), F32, kind="ExternalOutput").ap())
    fusion_kernel(nc, *args)
    r = run_bass_kernel_spmd(nc, [in_maps], core_ids=[0])
    return r.results[0]["out_0"]
```
